# Optimizing a Trainium2 kernel written in Bass

```python
import numpy as np
import jax
import jax.numpy as jnp

def _softmax(x, axis=-1):
    return jax.nn.softmax(x, axis=axis)

def _gelu(x):
    return jax.nn.gelu(x, approximate=True)

def _silu(x):
    return jax.nn.silu(x)

def _sigmoid(x):
    return jax.nn.sigmoid(x)

def _layernorm(x, axis=-1, eps=1e-05):
    m = jnp.mean(x, axis=axis, keepdims=True)
    v = jnp.var(x, axis=axis, keepdims=True)
    return (x - m) / jnp.sqrt(v + eps)

def _scatter_add(tgt, idx, src, axis=0):
    return tgt.at[idx].add(src)

def _segment_sum(src, seg, n):
    return jax.ops.segment_sum(src, seg, n)
kernel_name = 'mk_prb_d1_jaxref_r4_9699ae'

def setup_inputs(seed: int=0):
    np.random.seed(seed)
    _w = jnp.asarray

    def _L0_attn_setup():
        import jax, jax.numpy as jnp
        import numpy as np
        N_HEADS = 16
        D_MODEL = 256
        SEQ_LEN = 512
        BATCH = 4
        key = jax.random.key(seed)
        k1, k2, k3 = jax.random.split(key, 3)
        std = 1.0 / np.sqrt(D_MODEL)
        x = jax.random.normal(k1, (BATCH, SEQ_LEN, D_MODEL), dtype=jnp.float32)
        w_qkv = std * jax.random.normal(k2, (D_MODEL, 3 * D_MODEL), dtype=jnp.float32)
        w_o = std * jax.random.normal(k3, (D_MODEL, D_MODEL), dtype=jnp.float32)
        return {'x': x, 'w_qkv': w_qkv, 'w_o': w_o}
    _L0_attn_in = _L0_attn_setup()

    def _L0_ffn_setup():
        import jax, jax.numpy as jnp
        import numpy as np
        EPS = 1e-09
        key = jax.random.key(seed)
        k1, k2, k3, k4 = jax.random.split(key, 4)
        B, T, H, D, E = (2, 512, 256, 256, 8)
        x = jax.random.normal(k1, (B, T, H), dtype=jnp.float32)
        gate_w = jax.random.normal(k2, (E, H), dtype=jnp.float32) * 0.02
        gate_up_proj = jax.random.normal(k3, (E, H, 2 * D), dtype=jnp.float32) * 0.02
        down_proj = jax.random.normal(k4, (E, D, H), dtype=jnp.float32) * 0.02
        return {'x': x, 'gate_w': gate_w, 'gate_up_proj': gate_up_proj, 'down_proj': down_proj}
    _L0_ffn_in = _L0_ffn_setup()
    _d = {'L0_attn_x': _L0_attn_in['x'], 'L0_attn_w_qkv': _L0_attn_in['w_qkv'], 'L0_attn_w_o': _L0_attn_in['w_o'], 'L0_ffn_gate_w': _L0_ffn_in['gate_w'], 'L0_ffn_gate_up_proj': _L0_ffn_in['gate_up_proj'], 'L0_ffn_down_proj': _L0_ffn_in['down_proj']}
    _x0 = _d['L0_attn_x']
    _d['L0_attn_x'] = jax.random.normal(jax.random.fold_in(jax.random.key(seed), 1), (4, 2048, 256), dtype=_x0.dtype)
    del _x0
    return _d

def reference(L0_attn_x, L0_attn_w_qkv, L0_attn_w_o, L0_ffn_gate_w, L0_ffn_gate_up_proj, L0_ffn_down_proj):

    def _L0_attn_ref(x, w_qkv, w_o):
        import jax, jax.numpy as jnp
        import numpy as np
        N_HEADS = 16
        D_MODEL = 256
        SEQ_LEN = 512
        BATCH = 4
        *lead, seq_len, d_model = x.shape
        head_dim = d_model // N_HEADS
        qkv = x @ w_qkv
        qkv = qkv.reshape(*qkv.shape[:-1], N_HEADS, 3 * head_dim)
        qkv = jnp.einsum('...Thd->...hTd', qkv)
        q, k, v = jnp.split(qkv, 3, axis=-1)
        scores = jnp.einsum('...hqd,...hkd->...hqk', q, k) / np.sqrt(d_model).astype(x.dtype)
        causal = jnp.tri(seq_len, dtype=bool)
        scores = jnp.where(causal, scores, jnp.asarray(-1e+30, dtype=scores.dtype))
        attn = jax.nn.softmax(scores, axis=-1)
        out = jnp.einsum('...hqk,...hkd->...qhd', attn, v)
        out = out.reshape(*out.shape[:-2], d_model)
        return out @ w_o

    def _L0_ffn_ref(x, gate_w, gate_up_proj, down_proj):
        import jax, jax.numpy as jnp
        import numpy as np
        EPS = 1e-09
        B, T, H = x.shape
        E = gate_w.shape[0]
        top_k = 2
        hidden = x.reshape(-1, H)
        router_logits = hidden @ gate_w.T
        routing_weights = jax.nn.softmax(router_logits.astype(jnp.float32), axis=-1)
        topk_weights, topk_indices = jax.lax.top_k(routing_weights, top_k)
        topk_weights = topk_weights / (jnp.sum(topk_weights, axis=-1, keepdims=True) + EPS)
        N = hidden.shape[0]
        routed = jnp.zeros((N, E), dtype=router_logits.dtype)
        rows = jnp.arange(N)[:, None]
        routed = routed.at[rows, topk_indices].set(topk_weights.astype(router_logits.dtype))
        routed = routed / (jnp.sum(routed, axis=-1, keepdims=True) + EPS)
        routed = routed.astype(hidden.dtype)
        gate_up = jnp.einsum('th,ehq->teq', hidden, gate_up_proj)
        gate, up = jnp.split(gate_up, 2, axis=-1)
        expert_outputs = jnp.einsum('teq,eqh->teh', jax.nn.silu(gate) * up, down_proj)
        out = jnp.sum(expert_outputs * routed[:, :, None], axis=1)
        return out.reshape(B, T, H)
    x = L0_attn_x
    xn = _layernorm(x, axis=-1)
    x = x + _L0_attn_ref(xn, L0_attn_w_qkv, L0_attn_w_o) + _L0_ffn_ref(xn, L0_ffn_gate_w, L0_ffn_gate_up_proj, L0_ffn_down_proj)
    return x

_drawn_inputs = setup_inputs


def setup_inputs(seed=0):
    import zlib

    import numpy as np

    out = dict(_drawn_inputs(seed))
    spreads = {}
    factors = {'L0_ffn_gate_w': 5.39, 'L0_ffn_gate_up_proj': 4.695, 'L0_ffn_down_proj': 4.7}
    for name, (base, spread) in spreads.items():
        noise = np.random.default_rng([zlib.crc32(name.encode()), seed]).standard_normal(out[name].shape)
        drawn = base * np.exp(spread * noise) if base else spread * noise
        out[name] = jnp.asarray(drawn.astype(out[name].dtype))
    for name, factor in factors.items():
        out[name] = (out[name] * factor).astype(out[name].dtype)
    return out
```

```python
import concourse.bass as bass
from concourse import mybir
from contextlib import ExitStack

F32 = mybir.dt.float32
BF16 = mybir.dt.bfloat16
I32 = mybir.dt.int32
U32 = mybir.dt.uint32
ALU = mybir.AluOpType
ACT = mybir.ActivationFunctionType
AX = mybir.AxisListType


def wait_alone(eng, sem, value, passed):
    eng.wait_ge(sem, value)
    eng.sem_inc(passed, 1)


BATCH, T, D = 4, 2048, 256
HEADS, HD = 16, 16
TOK = BATCH * T
P = 128
KC = D // P
EXPERTS, FF = 8, 256
LN_EPS = 1e-5
ROUTE_EPS = 1e-9
NEG = -1e30
SCALE = 1.0 / 16.0

BLK = 512
JT = BLK // P
NBLK = TOK // BLK

SLOT_TILES = -(-(2 * TOK + EXPERTS * (P - 1)) // P)
SLOT_TILES += -SLOT_TILES % 4

GH = 4
HGS = HEADS // GH
GROUPS = BATCH * HGS
CH = 512
NCH = T // CH
QT = CH // P
VW = 32
Q_TERMS = [0, 0, 1, 1, 0, 2]
K_TERMS = [0, 1, 0, 1, 2, 0]
QK_ROWS = HD * len(Q_TERMS)
SHIFT_ROWS = 3
B_ROWS = QK_ROWS + SHIFT_ROWS

STEPS = [(c, kt) for c in range(NCH) for kt in range(QT * (c + 1))]
NSTEP = len(STEPS)
LAG = 2
RING = 4


def max_units():
    out = []
    for c in range(NCH):
        for r in range(QT):
            qt = QT * c + r
            for slot in range(c):
                out += [(c, slot, qt, [h], slot * CH, CH, False) for h in range(GH)]
            w = (r + 1) * P
            per = {1: 4, 2: 2, 3: 1, 4: 1}[r + 1]
            out += [(c, c, qt, list(range(h, h + per)), c * CH, w, True) for h in range(0, GH, per)]
    return out


UNITS = max_units()
NUNIT = len(UNITS)


def timetable(lead=78, shift_after=2, out_after=2):
    at = [[] for _ in range(NSTEP)]
    ends, done = [], 0
    for c, kt in STEPS:
        done += CH - P * max(0, kt - QT * c)
        ends.append(done)
    total = ends[-1]

    def put(t, kind, group, n):
        at[t % NSTEP].append((kind, group - t // NSTEP, n))

    work, t = 0, -NSTEP
    last = {}
    for n, (c, slot, qt, heads, k0, w, diag) in enumerate(UNITS):
        work += len(heads) * w // GH
        t = next(x for x in range(-NSTEP, NSTEP)
                 if ends[x % NSTEP] + total * (x // NSTEP) + lead * P >= work)
        put(t, "unit", 0, n)
        last[c] = t
    for c in range(NCH):
        put(last[c], "fold", 0, c)
        put(last[c] + shift_after, "shift", 0, c)
    for c in range(NCH):
        end = max(s for s, (x, _) in enumerate(STEPS) if x == c) + LAG
        put(end, "evac", 0, c)
        put(end + out_after, "norm", 0, c)
    for row in at:
        row.sort(key=lambda x: ({"unit": 0, "fold": 1, "evac": 2, "shift": 3, "norm": 4}[x[0]], x[1], x[2]))
    return at


TABLE = timetable()


def layernorm_qkv(nc, x, w_qkv, gate_w, xn_d, split_d, v_d, logits, ident):
    x_t = x.rearrange("b (n j p) d -> (b n) p j d", j=JT, p=P)
    xn_t = xn_d.rearrange("(n j p) d -> n p j d", j=JT, p=P)
    with ExitStack() as ctx:
        def sb(name, shape, dt=F32):
            return ctx.enter_context(nc.sbuf_tensor(name, shape, dt))

        def sem(name):
            return ctx.enter_context(nc.semaphore(name))

        w_raw = sb("w_raw", [P, KC, 3 * D])
        w_qk = sb("w_qk", [P, KC, 2, D])
        w_vg = sb("w_vg", [P, KC, D + EXPERTS])
        g_raw = sb("g_raw", [EXPERTS, D])
        x_sb = [sb(f"x_sb{u}", [P, JT, D]) for u in range(2)]
        xn_sb = [sb(f"xn_sb{u}", [P, JT, D]) for u in range(2)]
        xT = [sb(f"xT{u}", [P, KC, BLK]) for u in range(2)]
        stats = sb("stats", [P, JT, 6])
        mv = sb("mv", [P, JT, 2])
        veps = sb("veps", [P, JT])
        std = sb("std", [P, JT])
        inv = sb("inv", [P, JT])
        nwt = sb("nwt", [P, JT])
        nwt2 = sb("nwt2", [P, JT])
        rstd = sb("rstd", [P, JT])
        rest = sb("rest", [P, 4, BLK])
        parts = [sb(f"parts{u}", [P, 4, 3, BLK], BF16) for u in range(2)]
        v_sb = [sb(f"v_sb{u}", [P, HGS, JT, GH * VW]) for u in range(2)]
        pT = ctx.enter_context(nc.psum_tensor("pT", [P, KC, BLK], F32))
        pQK = [ctx.enter_context(nc.psum_tensor(f"pQK{o}", [P, BLK], F32)) for o in range(4)]
        pV = [ctx.enter_context(nc.psum_tensor(f"pV{o}", [P, BLK], F32)) for o in range(2)]

        passed = sem("passed")
        w_loaded = sem("w_loaded")
        w_ready = sem("w_ready")
        ident_zero = sem("ident_zero")
        ident_ready = sem("ident_ready")
        gateT_done = sem("gateT_done")
        gateT_copied = sem("gateT_copied")
        ones_zero = sem("ones_zero")
        v_pad = sem("v_pad")
        x_loaded = [sem(f"x_loaded{u}") for u in range(2)]
        stats_done = sem("stats_done")
        mv_done = sem("mv_done")
        veps_done = sem("veps_done")
        std_done = sem("std_done")
        inv_done = sem("inv_done")
        xn_done = sem("xn_done")
        xT_done = sem("xT_done")
        xT_copied = sem("xT_copied")
        qk_done = sem("qk_done")
        hi_done = sem("hi_done")
        rest_done = sem("rest_done")
        mid_done = sem("mid_done")
        lo_done = sem("lo_done")
        v_done = sem("v_done")
        v_copied = sem("v_copied")
        spilled = [sem(f"spilled{u}") for u in range(2)]
        SPILLS = 16 * 6

        block = ctx.enter_context(nc.Block())

        def every_block(eng, step):
            step(0, 0, 0)
            step(1, 1, 0)
            with eng.Fori(0, NBLK // 2 - 2) as i:
                step(2 * i + 2, 0, i + 1)
                step(2 * i + 3, 1, i + 1)
            step(NBLK - 2, 0, NBLK // 2 - 1)
            step(NBLK - 1, 1, NBLK // 2 - 1)

        def early(n):
            return isinstance(n, int) and n < 2

        def is_block(n, k):
            return isinstance(n, int) and n == k

        @block.sync
        def _(sp):
            sp.dma_start(x_sb[0][:, :, :], x_t[0]).then_inc(x_loaded[0], 16)
            sp.dma_start(w_raw[:, :, :], w_qkv.rearrange("(c p) n -> p c n", p=P)).then_inc(w_loaded, 16)
            sp.dma_start(g_raw[:, :], gate_w).then_inc(w_loaded, 16)
            sp.dma_start(x_sb[1][:, :, :], x_t[1]).then_inc(x_loaded[1], 16)

            def step(n, u, k):
                sp.wait_ge(xn_done, n + 1)
                sp.dma_start(xn_t[bass.ds(n, 1)].squeeze(0), xn_sb[u][:, :, :]).then_inc(spilled[u], 16)
                if not (isinstance(n, int) and n >= NBLK - 2):
                    sp.dma_start(x_sb[u][:, :, :], x_t[bass.ds(n + 2, 1)].squeeze(0)).then_inc(x_loaded[u], 16)
                for o in range(4):
                    side, half = o // 2, o % 2
                    sp.wait_ge(lo_done, 4 * n + o + 1)
                    sp.dma_start(split_d[:, side, half * P:half * P + P, bass.ds(n * BLK, BLK)]
                                 .rearrange("t r c -> r t c"), parts[u][:, o, :, :]).then_inc(spilled[u], 16)
                sp.wait_ge(v_copied, 4 * n + 4)
                sp.dma_start(v_d[:, :, bass.ds(n * JT, JT), :].rearrange("g p j w -> p g j w"),
                             v_sb[u][:, :, :, :]).then_inc(spilled[u], 16)

            every_block(sp, step)
            for u in range(2):
                sp.wait_ge(spilled[u], SPILLS * NBLK // 2)

        @block.gpsimd
        def _(pool):
            nc.gpsimd.memset(ident[:, :], 0.0).then_inc(ident_zero, 1)
            pool.wait_ge(ident_zero, 1)
            nc.gpsimd.affine_select(out=ident[:, :], in_=ident[:, :], compare_op=ALU.not_equal, fill=1.0,
                                    base=0, pattern=[[-1, P]], channel_multiplier=1).then_inc(ident_ready, 1)
            pool.wait_ge(w_loaded, 32)
            for c in range(KC):
                cols = w_raw[:, c, :].rearrange("p (h t d) -> p t h d", t=3, d=HD)
                for t in range(2):
                    nc.gpsimd.tensor_copy(w_qk[:, c, t, :].rearrange("p (h d) -> p h d", d=HD), cols[:, t])
                nc.gpsimd.tensor_copy(w_vg[:, c, 0:D].rearrange("p (h d) -> p h d", d=HD),
                                      cols[:, 2]).then_inc(w_ready, 1)
            for u in range(2):
                nc.gpsimd.memset(v_sb[u][:, :, :, :], 0.0).then_inc(ones_zero, 1)
            pool.wait_ge(ones_zero, 2)
            for u in range(2):
                nc.gpsimd.memset(v_sb[u][:, :, :, :].rearrange("p g j (h w) -> p (g j h) w", w=VW)
                                 [:, :, HD:HD + 1], 1.0).then_inc(v_pad, 1)

            def step(n, u, k):
                for o in range(4):
                    pool.wait_ge(mid_done, 4 * n + o + 1)
                    nc.gpsimd.tensor_tensor(parts[u][:, o, 2, :], rest[:, o, :], parts[u][:, o, 1, :],
                                            ALU.subtract).then_inc(lo_done, 1)

            every_block(pool, step)

        @block.vector
        def _(dve):
            dve.wait_ge(gateT_done, 1)
            nc.vector.tensor_copy(w_vg[:, :, D:D + EXPERTS],
                                  pV[0][:, 0:KC * EXPERTS].rearrange("p (c e) -> p c e", c=KC)).then_inc(gateT_copied, 1)

            def norm(n, u, k):
                dve.wait_ge(x_loaded[u], 16 * (k + 1))
                for j in range(JT):
                    last = nc.vector.bn_stats(stats[:, j, :], x_sb[u][:, j, :])
                last.then_inc(stats_done, 1)
                wait_alone(dve, stats_done, n + 1, passed)
                for j in range(JT):
                    last = nc.vector.bn_aggr(mv[:, j, :], stats[:, j, :])
                last.then_inc(mv_done, 1)
                dve.wait_ge(mv_done, n + 1)
                nc.vector.tensor_scalar(veps[:, :], mv[:, :, 1], LN_EPS, None, ALU.add).then_inc(veps_done, 1)
                dve.wait_ge(std_done, n + 1)
                nc.vector.reciprocal(inv[:, :], std[:, :]).then_inc(inv_done, 1)
                dve.wait_ge(inv_done, 4 * n + 1)
                nc.vector.tensor_tensor(nwt[:, :], inv[:, :], inv[:, :], ALU.mult).then_inc(inv_done, 1)
                dve.wait_ge(inv_done, 4 * n + 2)
                nc.vector.scalar_tensor_tensor(nwt2[:, :], nwt[:, :], -0.5, veps[:, :], ALU.mult, ALU.mult).then_inc(inv_done, 1)
                dve.wait_ge(inv_done, 4 * n + 3)
                nc.vector.scalar_tensor_tensor(rstd[:, :], nwt2[:, :], 1.5, inv[:, :], ALU.add, ALU.mult).then_inc(inv_done, 1)
                dve.wait_ge(inv_done, 4 * n + 4)
                if not early(n):
                    dve.wait_ge(spilled[u], SPILLS * k)
                for j in range(JT):
                    last = nc.vector.tensor_scalar(xn_sb[u][:, j, :], x_sb[u][:, j, :], mv[:, j, 0:1],
                                                   rstd[:, j:j + 1], ALU.subtract, ALU.mult)
                last.then_inc(xn_done, 1)

            norm(0, 0, 0)

            def step(n, u, k):
                if not is_block(n, NBLK - 1):
                    norm(n + 1, 1 - u, k + u)
                for o in range(4):
                    dve.wait_ge(hi_done, 4 * n + o + 1)
                    if not is_block(n, 0):
                        dve.wait_ge(lo_done, 4 * n + o - 3)
                    nc.vector.tensor_tensor(rest[:, o, :], pQK[o][:, :], parts[u][:, o, 0, :],
                                            ALU.subtract).then_inc(rest_done, 1)
                    dve.wait_ge(rest_done, 4 * n + o + 1)
                    nc.vector.tensor_copy(parts[u][:, o, 1, :], rest[:, o, :]).then_inc(mid_done, 1)

            every_block(dve, step)

        @block.scalar
        def _(act):
            def root(n):
                act.wait_ge(veps_done, n + 1)
                nc.scalar.activation(std[:, :], veps[:, :], ACT.Sqrt).then_inc(std_done, 1)

            def xT_copy(n, u):
                act.wait_ge(xT_done, n + 1)
                if not early(n):
                    act.wait_ge(v_done, 4 * n - 4)
                for c in range(KC):
                    last = nc.scalar.activation(xT[u][:, c, :], pT[:, c, :], ACT.Copy)
                last.then_inc(xT_copied, 1)

            root(0)
            xT_copy(0, 0)

            def step(n, u, k):
                if not is_block(n, NBLK - 1):
                    root(n + 1)
                if not early(n):
                    act.wait_ge(spilled[u], SPILLS * k)
                for o in range(4):
                    act.wait_ge(qk_done, 4 * n + o + 1)
                    nc.scalar.activation(parts[u][:, o, 0, :], pQK[o][:, :], ACT.Copy).then_inc(hi_done, 1)
                if not is_block(n, NBLK - 1):
                    xT_copy(n + 1, 1 - u)
                if is_block(n, 0):
                    act.wait_ge(v_pad, 2)
                for j in range(JT):
                    act.wait_ge(v_done, 4 * n + j + 1)
                    nc.scalar.activation(
                        v_sb[u][:, :, j, :].rearrange("p g (h w) -> p g h w", w=VW)[:, :, :, 0:HD],
                        pV[j % 2][:, 0:D].rearrange("p (g h d) -> p g h d", g=HGS, d=HD), ACT.Copy)
                    nc.scalar.activation(logits[:, bass.ds(n * JT + j, 1), :].squeeze(1),
                                         pV[j % 2][:, D:D + EXPERTS], ACT.Copy).then_inc(v_copied, 1)

            every_block(act, step)

        @block.tensor
        def _(pe):
            pe.wait_ge(ident_ready, 1)
            pe.wait_ge(w_loaded, 32)
            for c in range(KC):
                last = nc.tensor.transpose(pV[0][:, c * EXPERTS:(c + 1) * EXPERTS], g_raw[:, c * P:(c + 1) * P],
                                           ident[0:EXPERTS, 0:EXPERTS])
            last.then_inc(gateT_done, 1)

            def transposes(n, u):
                pe.wait_ge(xn_done, n + 1)
                if not is_block(n, 0):
                    pe.wait_ge(xT_copied, n)
                for c in range(KC):
                    for j in range(JT):
                        last = nc.tensor.transpose(pT[:, c, j * P:(j + 1) * P], xn_sb[u][:, j, c * P:(c + 1) * P],
                                                   ident[:, :])
                last.then_inc(xT_done, 1)

            transposes(0, 0)
            pe.wait_ge(w_ready, KC)
            pe.wait_ge(gateT_copied, 1)

            def step(n, u, k):
                pe.wait_ge(xT_copied, n + 1)
                for o in range(4):
                    side, half = o // 2, o % 2
                    if not is_block(n, 0):
                        pe.wait_ge(rest_done, 4 * n + o - 3)
                    for c in range(KC):
                        last = nc.tensor.matmul(pQK[o][:, :], w_qk[:, c, side, half * P:half * P + P],
                                                xT[u][:, c, :], start=c == 0, stop=c == KC - 1)
                    last.then_inc(qk_done, 1)
                if not is_block(n, NBLK - 1):
                    transposes(n + 1, 1 - u)
                for j in range(JT):
                    if not (is_block(n, 0) and j < 2):
                        pe.wait_ge(v_copied, 4 * n + j - 1)
                    for c in range(KC):
                        last = nc.tensor.matmul(pV[j % 2][:, 0:D + EXPERTS], xT[u][:, c, j * P:(j + 1) * P],
                                                w_vg[:, c, :], start=c == 0, stop=c == KC - 1)
                    last.then_inc(v_done, 1)

            every_block(pe, step)


def attention(nc, split_d, v_d, o_d, ident, slots, tokens, slot_d, preload):
    with ExitStack() as ctx:
        def sb(name, shape, dt=F32):
            return ctx.enter_context(nc.sbuf_tensor(name, shape, dt))

        def ps(name, shape, dt=F32):
            return ctx.enter_context(nc.psum_tensor(name, shape, dt))

        def sem(name):
            return ctx.enter_context(nc.semaphore(name))

        q_op = [sb(f"q_op{u}", [B_ROWS, GH, T], BF16) for u in range(2)]
        k_op = [sb(f"k_op{u}", [B_ROWS, GH, T], BF16) for u in range(2)]
        v_op = [sb(f"v_op{u}", [P, T // P, GH, VW]) for u in range(2)]
        prob = [sb(f"prob{r}", [P, GH, CH]) for r in range(RING)]
        ident_b = sb("ident_b", [P, P], BF16)
        mask_b = sb("mask_b", [P, P], BF16)
        part_max = [sb(f"part_max{u}", [P, GH, QT, NCH]) for u in range(2)]
        shift = sb("shift", [P, GH * QT])
        shift_r = sb("shift_r", [P, GH * QT])
        shift_r2 = sb("shift_r2", [P, GH * QT])
        shift_p = sb("shift_p", [P, GH, SHIFT_ROWS, QT], BF16)
        shiftT = sb("shiftT", [SHIFT_ROWS * GH * QT, P], BF16)
        oT_sb = sb("oT_sb", [P, CH])
        recip = sb("recip", [P, QT * GH])
        o_sb = [sb(f"o_sb{u}", [P, QT, GH * HD]) for u in range(2)]
        SENDS = 2 * TOK // P // GROUPS
        slot_now = [sb(f"slot_now{q}", [P, 1], I32) for q in range(SENDS)]
        token_now = [sb(f"token_now{q}", [P, 2], I32) for q in range(SENDS)]
        pS = [ps(f"pS{u}", [P, 2, CH]) for u in range(2)]
        pM = [ps(f"pM{u}", [P, CH]) for u in range(2)]
        pO = ps("pO", [P, CH])
        pX = ps("pX", [P, QT, GH, VW])
        pXs = pX[:, 0, :, :].rearrange("p h w -> p (h w)").bitcast(BF16)

        consts = sem("consts")
        passed = sem("passed")
        pe_passed = sem("pe_passed")
        consts_b = sem("consts_b")
        op_loaded = [sem(f"op_loaded{u}") for u in range(2)]
        v_loaded = [sem(f"v_loaded{u}") for u in range(2)]
        scores_done = sem("scores_done")
        exp_done = sem("exp_done")
        masked = sem("masked")
        pv_done = sem("pv_done")
        unit_done = sem("unit_done")
        unit_max = sem("unit_max")
        shift_max = sem("shift_max")
        shift_step = sem("shift_step")
        shiftT_done = sem("shiftT_done")
        shiftT_copied = sem("shiftT_copied")
        shift_loaded = [sem(f"shift_loaded{c}") for c in range(NCH)]
        o_copied = sem("o_copied")
        oT_done = sem("oT_done")
        recip_done = sem("recip_done")
        o_normed = sem("o_normed")
        o_stored = [sem(f"o_stored{u}") for u in range(2)]
        w_preloaded = sem("w_preloaded")
        slot_picked = sem("slot_picked")
        slot_sent = [sem(f"slot_sent{q}") for q in range(SENDS)]
        OPS = 16 * 2 * len(Q_TERMS)
        SHIFTS = 16 * GH

        block = ctx.enter_context(nc.Block())

        def every_period(eng, period):
            period(0, 0, 0, "first")
            with eng.Fori(0, GROUPS // 2 - 1) as i:
                period(2 * i + 1, 1, i, "inner")
                period(2 * i + 2, 0, i + 1, "inner")
            period(GROUPS - 1, 1, GROUPS // 2 - 1, "last")

        def items(s, where):
            for kind, rel, n in TABLE[s]:
                if where == "last" and rel > 0 or where == "first" and rel < 0:
                    continue
                yield kind, rel, n

        def before_first():
            return [(kind, n) for row in TABLE for kind, rel, n in row if rel == 1]

        def after_last():
            return [(kind, n) for row in TABLE for kind, rel, n in row if rel == -1]

        def n_before(kind, s):
            return sum(x[0] == kind for row in TABLE[:s] for x in row)

        @block.sync
        def _(sp):
            def load_qk(g, v, wait):
                if wait is not None:
                    sp.wait_ge(scores_done, wait)
                rows = bass.ds(g % HGS * (GH * HD), GH * HD)
                cols = bass.ds(g // HGS * T, T)
                for side, (op, terms) in enumerate(((q_op[v], Q_TERMS), (k_op[v], K_TERMS))):
                    for t, part in enumerate(terms):
                        sp.dma_start(op[t * HD:(t + 1) * HD, :, :],
                                     split_d[part, side, rows, cols].rearrange("(h d) c -> d h c", d=HD)
                                     ).then_inc(op_loaded[v], 16)

            def load_v(g, v, wait):
                if wait is not None:
                    sp.wait_ge(pv_done, wait)
                sp.dma_start(v_op[v][:, :, :, :].rearrange("p k h w -> p k (h w)"),
                             v_d[bass.ds(g % HGS, 1), :, bass.ds(g // HGS * (T // P), T // P), :].squeeze(0)
                             ).then_inc(v_loaded[v], 16)

            def send_shift(g, v, c):
                sp.wait_ge(shiftT_copied, NCH * g + c + 1)
                for h in range(GH):
                    sp.dma_start(q_op[v][QK_ROWS:B_ROWS, h, c * CH:(c + 1) * CH].rearrange("r (q p) -> r q p", p=P),
                                 shiftT[h * SHIFT_ROWS * QT:(h + 1) * SHIFT_ROWS * QT, :]).then_inc(shift_loaded[c], 16)

            def store(g, c):
                sp.wait_ge(o_normed, NCH * g + c + 1)
                sp.dma_start(
                    o_d[bass.ds(g // HGS * T + c * CH, CH), bass.ds(g % HGS * (GH * HD), GH * HD)]
                    .rearrange("(q p) w -> p q w", p=P), o_sb[c % 2][:, :, :]).then_inc(o_stored[c % 2], 16)

            load_qk(0, 0, None)
            load_v(0, 0, None)
            (w_o_sb, w_o), *expert_weights = preload
            sp.dma_start(w_o_sb[:, :, :], w_o.rearrange("(c p) n -> p c n", p=P)).then_inc(w_preloaded, 16)
            for to, w in expert_weights:
                for c in range(KC):
                    sp.dma_start(to[:, c, :].rearrange("p (e n) -> p e n", e=EXPERTS),
                                 w[:, c * P:(c + 1) * P, :].rearrange("e p n -> p e n")).then_inc(w_preloaded, 16)
            for kind, n in before_first():
                if kind == "shift":
                    send_shift(0, 0, n)

            def period(g, u, k, where):
                for s in range(NSTEP):
                    if s == 0 and where != "last":
                        load_qk(g + 1, 1 - u, None if where == "first" else 2 * NSTEP * g)
                    if s == LAG + 1 and where != "last":
                        load_v(g + 1, 1 - u, None if where == "first" else NSTEP * g)
                    for kind, rel, n in items(s, where):
                        if kind == "shift":
                            send_shift(g + rel, (u + rel) % 2, n)
                        if kind == "norm":
                            store(g + rel, n)

            every_period(sp, period)
            for kind, n in after_last():
                if kind == "norm":
                    store(GROUPS - 1, n)
            for u in range(2):
                sp.wait_ge(o_stored[u], 16 * GROUPS * NCH // 2)
            sp.wait_ge(w_preloaded, 16 * 5)

        @block.gpsimd
        def _(pool):
            nc.gpsimd.memset(ident_b[:, :], 0.0).then_inc(consts, 1)
            nc.gpsimd.memset(mask_b[:, :], 0.0).then_inc(consts, 1)
            pool.wait_ge(consts, 2)
            nc.gpsimd.affine_select(out=ident_b[:, :], in_=ident_b[:, :], compare_op=ALU.not_equal, fill=1.0,
                                    base=0, pattern=[[-1, P]], channel_multiplier=1).then_inc(consts_b, 1)
            nc.gpsimd.affine_select(out=mask_b[:, :], in_=mask_b[:, :], compare_op=ALU.is_ge, fill=NEG,
                                    base=0, pattern=[[-1, P]], channel_multiplier=1).then_inc(consts_b, 1)
            def byhead(x):
                return x[:, :].rearrange("p (h q) -> p h q", h=GH)

            def split_shift(g, c):
                at = 5 * (NCH * g + c)
                if not (isinstance(g, int) and g == 0 and c == 0):
                    pool.wait_ge(shiftT_done, NCH * g + c)
                wait_alone(pool, shift_max, NCH * g + c + 1, passed)
                nc.gpsimd.tensor_copy(shift_p[:, :, 0, :], byhead(shift)).then_inc(shift_step, 1)
                pool.wait_ge(shift_step, at + 1)
                nc.gpsimd.tensor_tensor(byhead(shift_r), byhead(shift), shift_p[:, :, 0, :], ALU.subtract).then_inc(shift_step, 1)
                wait_alone(pool, shift_step, at + 2, passed)
                nc.gpsimd.tensor_copy(shift_p[:, :, 1, :], byhead(shift_r)).then_inc(shift_step, 1)
                pool.wait_ge(shift_step, at + 3)
                nc.gpsimd.tensor_tensor(byhead(shift_r2), byhead(shift_r), shift_p[:, :, 1, :], ALU.subtract).then_inc(shift_step, 1)
                wait_alone(pool, shift_step, at + 4, passed)
                nc.gpsimd.tensor_copy(shift_p[:, :, 2, :], byhead(shift_r2)).then_inc(shift_step, 1)

            def place(g, q, where):
                tile, rank = g * (SENDS // 2) + q // 2, q % 2
                if where != "first":
                    wait_alone(pool, slot_sent[q], 16 * g, passed)
                nc.gpsimd.tensor_copy(slot_now[q][:, :], slots[:, bass.ds(tile, 1), rank])
                nc.gpsimd.tensor_copy(token_now[q][:, :], tokens[:, bass.ds(tile, 1), rank, :].squeeze(1)).then_inc(slot_picked, 1)
                wait_alone(pool, slot_picked, SENDS * g + q + 1, passed)
                nc.gpsimd.indirect_dma_start(slot_d, bass.IndirectOffsetOnAxis(slot_now[q][:, 0:1].bitcast(U32), 0),
                                             token_now[q][:, :], None,
                                             bounds_check=SLOT_TILES * P - 1).then_inc(slot_sent[q], 16)

            for kind, n in before_first():
                if kind == "fold":
                    split_shift(0, n)

            def period(g, u, k, where):
                for s, (c, kt) in enumerate(STEPS):
                    if kt >= QT * c:
                        w0 = (kt - QT * c) * P
                        wait_alone(pool, exp_done, 2 * (NSTEP * g + s) + 2, passed)
                        tri = prob[s % RING][:, :, w0:w0 + P]
                        nc.gpsimd.affine_select(out=tri, in_=tri, compare_op=ALU.is_ge, fill=0.0, base=0,
                                                pattern=[[0, GH], [1, P]], channel_multiplier=-1).then_inc(masked, 1)
                    for kind, rel, n in items(s, where):
                        if kind == "fold":
                            split_shift(g + rel, n)
                    if s % 4 == 2 and s // 4 < SENDS:
                        place(g, s // 4, where)

            every_period(pool, period)
            for q in range(SENDS):
                pool.wait_ge(slot_sent[q], 16 * GROUPS)

        @block.vector
        def _(dve):
            def unit(g, n):
                c, slot, qt, heads, k0, w, diag = UNITS[n]
                dve.wait_ge(unit_done, NUNIT * g + n + 1)
                nc.vector.tensor_reduce(part_max[c % 2][:, heads[0]:heads[-1] + 1, qt % QT, slot:slot + 1],
                                        pM[n % 2][:, 0:len(heads) * w].rearrange("p (h k) -> p h k", k=w),
                                        AX.X, ALU.max).then_inc(unit_max, 1)

            def fold(g, c):
                upto = max(n for n, x in enumerate(UNITS) if x[0] == c) + 1
                dve.wait_ge(unit_max, NUNIT * g + upto)
                if not (isinstance(g, int) and g == 0 and c == 0):
                    dve.wait_ge(shift_step, 5 * (NCH * g + c))
                nc.vector.tensor_reduce(shift[:, :].rearrange("p (h q) -> p h q", h=GH),
                                        part_max[c % 2][:, :, :, 0:c + 1], AX.X, ALU.max,
                                        negate=True).then_inc(shift_max, 1)

            def norm(g, c):
                e = NCH * g + c
                dve.wait_ge(oT_done, e + 1)
                nc.vector.reciprocal(recip[:, :], pX[:, :, :, HD].rearrange("p q h -> p (q h)")).then_inc(recip_done, 1)
                dve.wait_ge(recip_done, e + 1)
                if isinstance(g, int) and g == 0:
                    if c >= 2:
                        dve.wait_ge(o_stored[c % 2], 16 * (c // 2))
                else:
                    dve.wait_ge(o_stored[c % 2], 16 * (2 * g + c // 2))
                nc.vector.tensor_tensor(
                    o_sb[c % 2][:, :, :].rearrange("p q (h d) -> p (q h) d", h=GH),
                    pX[:, :, :, 0:HD].rearrange("p q h d -> p (q h) d"),
                    recip[:, :].unsqueeze(2).to_broadcast([P, QT * GH, HD]), ALU.mult).then_inc(o_normed, 1)

            for u in range(2):
                nc.vector.memset(k_op[u][QK_ROWS:B_ROWS, :, :], 1.0).then_inc(consts_b, 1)
            for kind, n in before_first():
                if kind == "unit":
                    unit(0, n)
                if kind == "fold":
                    fold(0, n)

            def period(g, u, k, where):
                for s in range(NSTEP):
                    for kind, rel, n in items(s, where):
                        if kind == "unit":
                            unit(g + rel, n)
                        if kind == "fold":
                            fold(g + rel, n)
                        if kind == "norm":
                            norm(g + rel, n)

            every_period(dve, period)
            for kind, n in after_last():
                if kind == "norm":
                    norm(GROUPS - 1, n)

        @block.scalar
        def _(act):
            def shift_copy(g, c):
                act.wait_ge(shiftT_done, NCH * g + c + 1)
                if not (isinstance(g, int) and g == 0 and c == 0):
                    before = (g, c - 1) if c else (g - 1, NCH - 1)
                    act.wait_ge(shift_loaded[before[1]], SHIFTS * (before[0] + 1))
                nc.scalar.activation(shiftT[:, :], pXs[0:SHIFT_ROWS * GH * QT, 0:P], ACT.Copy).then_inc(shiftT_copied, 1)

            def evac(g, c):
                e = NCH * g + c
                at = LAG + max(s for s, (x, _) in enumerate(STEPS) if x == c)
                act.wait_ge(pv_done, NSTEP * g + at - LAG + 1)
                if not (isinstance(g, int) and g == 0 and c == 0):
                    act.wait_ge(oT_done, e)
                nc.scalar.activation(oT_sb[:, :], pO[:, :], ACT.Copy).then_inc(o_copied, 1)

            for kind, n in before_first():
                if kind == "shift":
                    shift_copy(0, n)

            def period(g, u, k, where):
                for s, (c, kt) in enumerate(STEPS):
                    w0 = P * max(0, kt - QT * c)
                    if not (where == "first" and s < RING):
                        act.wait_ge(pv_done, NSTEP * g + s - RING + 1)
                    for pair in range(2):
                        act.wait_ge(scores_done, 2 * (NSTEP * g + s) + pair + 1)
                        nc.scalar.activation(prob[s % RING][:, 2 * pair:2 * pair + 2, w0:CH],
                                             pS[pair][:, :, w0:CH], ACT.Exp, scale=SCALE).then_inc(exp_done, 1)
                    for kind, rel, n in items(s, where):
                        if kind == "shift":
                            shift_copy(g + rel, n)
                        if kind == "evac":
                            evac(g + rel, n)

            every_period(act, period)
            for kind, n in after_last():
                if kind == "evac":
                    evac(GROUPS - 1, n)

        @block.tensor
        def _(pe):
            pe.wait_ge(consts_b, 4)

            def unit(g, v, kv, n):
                c, slot, qt, heads, k0, w, diag = UNITS[n]
                if n == 0:
                    pe.wait_ge(op_loaded[v], OPS * (kv + 1))
                if not (isinstance(g, int) and g == 0 and n < 2):
                    pe.wait_ge(unit_max, NUNIT * g + n - 1)
                for x, h in enumerate(heads):
                    last = nc.tensor.matmul(pM[n % 2][:, x * w:(x + 1) * w], q_op[v][0:QK_ROWS, h, qt * P:(qt + 1) * P],
                                            k_op[v][0:QK_ROWS, h, k0:k0 + w], start=True, stop=not diag)
                    if diag:
                        last = nc.tensor.matmul(pM[n % 2][:, (x + 1) * w - P:(x + 1) * w], ident_b[:, :], mask_b[:, :],
                                                start=False, stop=True)
                last.then_inc(unit_done, 1)

            def scores(g, u, s, pair, where):
                c, kt = STEPS[s]
                w0 = P * max(0, kt - QT * c)
                if kt == 0 and pair == 0:
                    pe.wait_ge(shift_loaded[c], SHIFTS * (g + 1))
                if not (where == "first" and s == 0):
                    pe.wait_ge(exp_done, 2 * (NSTEP * g + s) + pair - 1)
                for x in range(2):
                    h = 2 * pair + x
                    last = nc.tensor.matmul(pS[pair][:, x, w0:CH], k_op[u][:, h, kt * P:(kt + 1) * P],
                                            q_op[u][:, h, c * CH + w0:(c + 1) * CH], start=True, stop=True)
                last.then_inc(scores_done, 1)

            def values(g, u, k, s, half):
                c, kt = STEPS[s]
                w0 = P * max(0, kt - QT * c)
                cols = [(w0, CH)] if CH - w0 <= CH // 2 else [(w0, CH // 2), (CH // 2, CH)]
                if half >= len(cols):
                    return
                if half == 1:
                    product(u, s, *cols[1], True)
                    return
                if s == 0:
                    pe.wait_ge(v_loaded[u], 16 * (k + 1))
                if kt >= QT * c:
                    pe.wait_ge(masked, NCH * QT * g + QT * c + kt - QT * c + 1)
                else:
                    pe.wait_ge(exp_done, 2 * (NSTEP * g + s) + 2)
                if kt == 0 and not (isinstance(g, int) and g == 0 and c == 0):
                    pe.wait_ge(o_copied, NCH * g + c)
                product(u, s, *cols[0], len(cols) == 1)

            def product(u, s, a, b, ends):
                c, kt = STEPS[s]
                for h in range(GH):
                    last = nc.tensor.matmul(pO[h * VW:(h + 1) * VW, a:b], v_op[u][:, kt, h, :],
                                            prob[s % RING][:, h, a:b], start=kt == 0 and a == 0,
                                            stop=kt == QT * (c + 1) - 1, skip_group_check=True,
                                            tile_position=(0, h * VW))
                if ends:
                    last.then_inc(pv_done, 1)

            order = [(kind, n, rel) for row in TABLE for kind, rel, n in row if kind in ("shift", "norm")]

            def shiftT_step(g, c, norms):
                pe.wait_ge(shift_step, 5 * (NCH * g + c) + 5)
                if norms is not None:
                    pe.wait_ge(o_normed, norms)
                if not (isinstance(g, int) and g == 0 and c == 0):
                    wait_alone(pe, shiftT_copied, NCH * g + c, pe_passed)
                nc.tensor.transpose(pXs[0:SHIFT_ROWS * GH * QT, 0:P], shift_p[:, :, :, :].rearrange("p h r q -> p (h r q)"),
                                    ident_b[:, :]).then_inc(shiftT_done, 1)

            def oT_step(g, c, shifts):
                e = NCH * g + c
                pe.wait_ge(o_copied, e + 1)
                pe.wait_ge(shiftT_copied, shifts)
                if not (isinstance(g, int) and g == 0 and c == 0):
                    pe.wait_ge(o_normed, e)
                for q in range(QT):
                    last = nc.tensor.transpose(pX[:, q, :, :].rearrange("p h w -> p (h w)"),
                                               oT_sb[:, q * P:(q + 1) * P], ident[:, :])
                last.then_inc(oT_done, 1)

            for kind, n in before_first():
                if kind == "unit":
                    unit(0, 0, 0, n)
                if kind == "shift":
                    shiftT_step(0, n, None)

            def period(g, u, k, where):
                for s in range(NSTEP):
                    todo = [(rel, n) for kind, rel, n in items(s, where) if kind == "unit"]
                    for slot in range(4):
                        for rel, n in todo[len(todo) * slot // 4:len(todo) * (slot + 1) // 4]:
                            unit(g + rel, (u + rel) % 2, k + (u if rel else 0), n)
                        if slot < 2:
                            scores(g, u, s, slot, where)
                        elif s >= LAG:
                            values(g, u, k, s - LAG, slot - 2)
                        elif where != "first":
                            values(g - 1, 1 - u, k - (1 - u), NSTEP + s - LAG, slot - 2)
                    for kind, rel, n in items(s, where):
                        if kind == "shift":
                            x = order.index(("shift", n, rel))
                            left = [(m, r) for knd, m, r in order[:x] if knd == "norm"]
                            if left:
                                m, r = left[-1]
                                norms = NCH * (g + r) + m + 1
                                if where == "first" and r < 0:
                                    norms = None
                            else:
                                m, r = [(m, r) for knd, m, r in order if knd == "norm"][-1]
                                norms = None if where == "first" else NCH * (g - 1 + r) + m + 1
                            shiftT_step(g + rel, n, norms)
                        if kind == "norm":
                            x = order.index(("norm", n, rel))
                            left = [(m, r) for knd, m, r in order[:x] if knd == "shift" and not (where == "last" and r > 0)]
                            if left:
                                m, r = left[-1]
                                shifts = NCH * (g + r) + m + 1
                            else:
                                m, r = [(m, r) for knd, m, r in order if knd == "shift"][-1]
                                shifts = NCH * (g - 1 + r) + m + 1
                            oT_step(g + rel, n, shifts)

            every_period(pe, period)
            for s in range(NSTEP - LAG, NSTEP):
                for half in range(2):
                    values(GROUPS - 1, 1, GROUPS // 2 - 1, s, half)
            for kind, n in after_last():
                if kind == "norm":
                    oT_step(GROUPS - 1, n, NCH * GROUPS)


def route(nc, logits, weights, slots, tokens, tile_expert, slot_d):
    NT = TOK // P
    with ExitStack() as ctx:
        def sb(name, shape, dt=F32):
            return ctx.enter_context(nc.sbuf_tensor(name, shape, dt))

        def sem(name):
            return ctx.enter_context(nc.semaphore(name))

        full = [P, NT, EXPERTS]
        e_int = sb("e_int", full, I32)
        e_less = sb("e_less", full)
        z = sb("z", full)
        ez = sb("ez", full)
        prb = sb("prb", full)
        eq = sb("eq", full)
        cand = sb("cand", full)
        hot = [sb(f"hot{r}", full) for r in range(2)]
        best = [sb(f"best{r}", [P, NT]) for r in range(2)]
        first = sb("first", [P, NT])
        mx = sb("mx", [P, NT])
        total = sb("total", [P, NT])
        inv = sb("inv_total", [P, NT])
        tk = [sb(f"tk{r}", [P, NT]) for r in range(2)]
        sel = sb("sel", full)
        zero = sb("zero", [P, NT])
        cum = sb("cum", [P, EXPERTS, NT])
        tiles_i = sb("tiles_i", [P, EXPERTS], I32)
        tiles_i2 = sb("tiles_i2", [P, EXPERTS], I32)
        tiles_f = sb("tiles_f", [P, EXPERTS])
        ends = sb("ends", [P, EXPERTS])
        begins = sb("begins", [P, EXPERTS])
        pos = sb("pos", full)
        slot_f = sb("slot_f", [P, NT])
        lower = sb("lower", [P, P])
        ones = sb("ones", [P, P])
        pad = sb("pad", [P, SLOT_TILES, 2], I32)
        j_int = sb("j_int", [1, SLOT_TILES, EXPERTS], I32)
        j_f = sb("j_f", [1, SLOT_TILES, EXPERTS])
        j_ge = sb("j_ge", [1, SLOT_TILES, EXPERTS])
        j_e = sb("j_e", [1, SLOT_TILES])
        pBefore = ctx.enter_context(nc.psum_tensor("pBefore", full, F32))
        pTile = ctx.enter_context(nc.psum_tensor("pTile", full, F32))

        made = sem("made")
        filled = sem("filled")
        chain = sem("chain")
        z_done = sem("z_done")
        ez_done = sem("ez_done")
        sel_done = sem("sel_done")
        counted = sem("counted")
        pad_sent = sem("pad_sent")
        block = ctx.enter_context(nc.Block())

        def over_experts(x):
            return x[:, :].unsqueeze(2).to_broadcast(full)

        @block.gpsimd
        def _(pool):
            nc.gpsimd.iota(e_int[:, :, :], [[0, NT], [1, EXPERTS]], base=-EXPERTS, channel_multiplier=0).then_inc(made, 1)
            nc.gpsimd.iota(j_int[:, :, :], [[1, SLOT_TILES], [0, EXPERTS]], base=0, channel_multiplier=0).then_inc(made, 1)
            nc.gpsimd.memset(ones[:, :], 1.0).then_inc(made, 1)
            nc.gpsimd.memset(lower[:, :], 1.0).then_inc(made, 1)
            nc.gpsimd.memset(zero[:, :], 0.0).then_inc(made, 1)
            nc.gpsimd.iota(tokens[:, :, :, 0], [[P, NT], [0, 2]], base=0, channel_multiplier=1).then_inc(made, 1)
            nc.gpsimd.iota(tokens[:, :, :, 1], [[P, NT], [TOK, 2]], base=0, channel_multiplier=1).then_inc(made, 1)
            nc.gpsimd.iota(pad[:, :, :], [[0, SLOT_TILES], [2 * TOK, 2]], base=0, channel_multiplier=0).then_inc(made, 1)
            pool.wait_ge(made, 4)
            nc.gpsimd.affine_select(out=lower[:, :], in_=lower[:, :], compare_op=ALU.is_gt, fill=0.0, base=0,
                                    pattern=[[1, P]], channel_multiplier=-1).then_inc(filled, 1)

        @block.sync
        def _(sp):
            sp.wait_ge(made, 8)
            sp.dma_start(slot_d.rearrange("(p n) c -> p (n c)", p=P),
                         pad[:, :, :].rearrange("p n c -> p (n c)")).then_inc(pad_sent, 16)
            sp.wait_ge(pad_sent, 16)

        @block.scalar
        def _(act):
            act.wait_ge(z_done, 1)
            nc.scalar.activation(ez[:, :, :], z[:, :, :], ACT.Exp).then_inc(ez_done, 1)

        @block.tensor
        def _(pe):
            pe.wait_ge(filled, 1)
            pe.wait_ge(made, 8)
            pe.wait_ge(sel_done, 1)
            for out, lhsT in ((pBefore, lower), (pTile, ones)):
                nc.tensor.matmul(out[:, :, :].rearrange("p t e -> p (t e)"), lhsT[:, :],
                                 sel[:, :, :].rearrange("p t e -> p (t e)"), start=True, stop=True).then_inc(counted, 1)

        @block.vector
        def _(dve):
            done = [0]

            def link(ins):
                done[0] += 1
                ins.then_inc(chain, 1)
                dve.wait_ge(chain, done[0])

            V = nc.vector
            dve.wait_ge(made, 8)
            link(V.tensor_copy(e_less[:, :, :], e_int[:, :, :]))
            link(V.tensor_reduce(mx[:, :], logits[:, :, :], AX.X, ALU.max))
            V.tensor_tensor(z[:, :, :], logits[:, :, :], over_experts(mx), ALU.subtract).then_inc(z_done, 1)
            dve.wait_ge(ez_done, 1)
            link(V.tensor_reduce(total[:, :], ez[:, :, :], AX.X, ALU.add))
            link(V.reciprocal(inv[:, :], total[:, :]))
            link(V.tensor_tensor(prb[:, :, :], ez[:, :, :], over_experts(inv), ALU.mult))
            for r in range(2):
                link(V.tensor_reduce(best[r][:, :], prb[:, :, :], AX.X, ALU.max))
                link(V.tensor_tensor(eq[:, :, :], prb[:, :, :], over_experts(best[r]), ALU.is_equal))
                link(V.tensor_tensor(cand[:, :, :], eq[:, :, :], e_less[:, :, :], ALU.mult))
                link(V.tensor_reduce(first[:, :], cand[:, :, :], AX.X, ALU.min))
                link(V.tensor_tensor(hot[r][:, :, :], e_less[:, :, :], over_experts(first), ALU.is_equal))
                if r == 0:
                    link(V.scalar_tensor_tensor(prb[:, :, :], hot[0][:, :, :], -2.0, prb[:, :, :], ALU.mult, ALU.add))
            V.tensor_tensor(sel[:, :, :], hot[0][:, :, :], hot[1][:, :, :], ALU.add).then_inc(sel_done, 1)
            link(V.tensor_tensor(total[:, :], best[0][:, :], best[1][:, :], ALU.add))
            link(V.tensor_scalar(total[:, :], total[:, :], ROUTE_EPS, None, ALU.add))
            link(V.reciprocal(inv[:, :], total[:, :]))
            for r in range(2):
                link(V.tensor_tensor(tk[r][:, :], best[r][:, :], inv[:, :], ALU.mult))
            link(V.tensor_tensor(total[:, :], tk[0][:, :], tk[1][:, :], ALU.add))
            link(V.tensor_scalar(total[:, :], total[:, :], ROUTE_EPS, None, ALU.add))
            link(V.reciprocal(inv[:, :], total[:, :]))
            for r in range(2):
                link(V.tensor_tensor(weights[:, r, :], tk[r][:, :], inv[:, :], ALU.mult))
            dve.wait_ge(counted, 2)
            for e in range(EXPERTS):
                link(V.tensor_tensor_scan(cum[:, e, :], pTile[:, :, e], zero[:, :], 0.0, ALU.add, ALU.add))
            link(V.tensor_scalar(tiles_i[:, :], cum[:, :, NT - 1], float(P - 1), None, ALU.add))
            link(V.tensor_scalar(tiles_i2[:, :], tiles_i[:, :], 7, None, ALU.logical_shift_right))
            link(V.tensor_copy(tiles_f[:, :], tiles_i2[:, :]))
            link(V.tensor_tensor_scan(ends[:, :], tiles_f[:, :], zero[:, 0:EXPERTS], 0.0, ALU.add, ALU.add))
            link(V.tensor_tensor(begins[:, :], ends[:, :], tiles_f[:, :], ALU.subtract))
            link(V.tensor_scalar(begins[:, :], begins[:, :], float(P), None, ALU.mult))
            link(V.tensor_tensor(pos[:, :, :], cum[:, :, :].rearrange("p e t -> p t e"), pTile[:, :, :], ALU.subtract))
            link(V.tensor_tensor(pos[:, :, :], pos[:, :, :], pBefore[:, :, :], ALU.add))
            link(V.tensor_tensor(pos[:, :, :], pos[:, :, :], begins[:, :].unsqueeze(1).to_broadcast(full), ALU.add))
            for r in range(2):
                link(V.tensor_tensor(cand[:, :, :], pos[:, :, :], hot[r][:, :, :], ALU.mult))
                link(V.tensor_reduce(slot_f[:, :], cand[:, :, :], AX.X, ALU.add))
                link(V.tensor_copy(slots[:, :, r], slot_f[:, :]))
            link(V.tensor_copy(j_f[:, :, :], j_int[:, :, :]))
            link(V.tensor_tensor(j_ge[:, :, :], j_f[:, :, :],
                                 ends[0:1, :].unsqueeze(1).to_broadcast([1, SLOT_TILES, EXPERTS]), ALU.is_ge))
            link(V.tensor_reduce(j_e[:, :], j_ge[:, :, :], AX.X, ALU.add))
            link(V.tensor_scalar(j_e[:, :], j_e[:, :], float(EXPERTS - 1), None, ALU.min))
            link(V.tensor_copy(tile_expert[:, :], j_e[:, :]))


def project(nc, x, o_d, w_o_sb, acc, ident):
    x_t = x.rearrange("b (n j p) d -> (b n) p j d", j=JT, p=P)
    o_t = o_d.rearrange("(n j p) d -> n p j d", j=JT, p=P)
    with ExitStack() as ctx:
        def sem(name):
            return ctx.enter_context(nc.semaphore(name))

        o_in = [ctx.enter_context(nc.sbuf_tensor(f"o_in{u}", [P, JT, D], F32)) for u in range(2)]
        oT = [ctx.enter_context(nc.sbuf_tensor(f"oT{u}", [P, KC, BLK], F32)) for u in range(2)]
        pOT = [ctx.enter_context(nc.psum_tensor(f"pOT{u}", [P, KC, BLK], F32)) for u in range(2)]
        pP = [ctx.enter_context(nc.psum_tensor(f"pP{u}", [P, 2, D], F32)) for u in range(2)]
        x_in = sem("x_in")
        o_loaded = [sem(f"o_loaded{u}") for u in range(2)]
        o_trans = sem("o_trans")
        o_evac = sem("o_evac")
        proj_done = sem("proj_done")
        proj_added = sem("proj_added")
        block = ctx.enter_context(nc.Block())

        def every_block(eng, step):
            step(0, 0, 0)
            step(1, 1, 0)
            with eng.Fori(0, NBLK // 2 - 2) as i:
                step(2 * i + 2, 0, i + 1)
                step(2 * i + 3, 1, i + 1)
            step(NBLK - 2, 0, NBLK // 2 - 1)
            step(NBLK - 1, 1, NBLK // 2 - 1)

        def is_block(n, k):
            return isinstance(n, int) and n == k

        @block.sync
        def _(sp):
            for n in range(4):
                sp.dma_start(acc[:, 16 * n:16 * n + 16, :].rearrange("p (m j) d -> p m j d", j=JT),
                             x_t[4 * n:4 * n + 4].rearrange("m p j d -> p m j d")).then_inc(x_in, 16)
                if n == 0:
                    for u in range(2):
                        sp.dma_start(o_in[u][:, :, :], o_t[u]).then_inc(o_loaded[u], 16)

            def step(n, u, k):
                if not (isinstance(n, int) and n >= NBLK - 2):
                    sp.wait_ge(o_trans, n + 1)
                    sp.dma_start(o_in[u][:, :, :], o_t[bass.ds(n + 2, 1)].squeeze(0)).then_inc(o_loaded[u], 16)

            every_block(sp, step)

        @block.tensor
        def _(pe):
            def trans(n, u, k):
                pe.wait_ge(o_loaded[u], 16 * (k + 1))
                if not (isinstance(n, int) and n < 2):
                    pe.wait_ge(o_evac, n - 1)
                for c in range(KC):
                    for j in range(JT):
                        last = nc.tensor.transpose(pOT[u][:, c, j * P:(j + 1) * P], o_in[u][:, j, c * P:(c + 1) * P],
                                                   ident[:, :])
                last.then_inc(o_trans, 1)

            trans(0, 0, 0)

            def step(n, u, k):
                if not is_block(n, NBLK - 1):
                    trans(n + 1, 1 - u, k + u)
                pe.wait_ge(o_evac, n + 1)
                for m in range(2):
                    if not is_block(n, 0):
                        pe.wait_ge(proj_added, 2 * n + m - 1)
                    for j in range(2):
                        for c in range(KC):
                            q = 2 * m + j
                            last = nc.tensor.matmul(pP[m][:, j, :], oT[u][:, c, q * P:(q + 1) * P], w_o_sb[:, c, :],
                                                    start=c == 0, stop=c == KC - 1)
                    last.then_inc(proj_done, 1)

            every_block(pe, step)

        @block.scalar
        def _(act):
            def step(n, u, k):
                act.wait_ge(o_trans, n + 1)
                if not (isinstance(n, int) and n < 2):
                    act.wait_ge(proj_done, 2 * n - 2)
                for c in range(KC):
                    last = nc.scalar.activation(oT[u][:, c, :], pOT[u][:, c, :], ACT.Copy)
                last.then_inc(o_evac, 1)

            every_block(act, step)

        @block.vector
        def _(dve):
            dve.wait_ge(x_in, 64)

            def step(n, u, k):
                for m in range(2):
                    dve.wait_ge(proj_done, 2 * n + m + 1)
                    part = acc[:, bass.ds(n * JT + 2 * m, 2), :]
                    nc.vector.tensor_tensor(part, pP[m][:, :, :], part, ALU.add).then_inc(proj_added, 1)

            every_block(dve, step)


def experts(nc, xn_d, slot_d, tile_expert, w_gu, w_dn, y_d, ident):
    GI = 4
    with ExitStack() as ctx:
        def sb(name, shape, dt=F32):
            return ctx.enter_context(nc.sbuf_tensor(name, shape, dt))

        def sem(name):
            return ctx.enter_context(nc.semaphore(name))

        src = [sb(f"src{r}", [P, 2], I32) for r in range(GI)]
        dst = [sb(f"dst{r}", [P, 2], I32) for r in range(GI)]
        xg = [sb(f"xg{r}", [P, D]) for r in range(GI)]
        xgT = [sb(f"xgT{u}", [P, KC, P]) for u in range(2)]
        gate = [sb(f"gate{u}", [P, FF]) for u in range(2)]
        hid = [sb(f"hid{u}", [P, FF]) for u in range(2)]
        hidT = [sb(f"hidT{u}", [P, KC, P]) for u in range(2)]
        y = [sb(f"y{r}", [P, D]) for r in range(GI)]
        pXT = ctx.enter_context(nc.psum_tensor("pXT", [P, KC, P], F32))
        pHT = ctx.enter_context(nc.psum_tensor("pHT", [P, KC, P], F32))
        pGU = [ctx.enter_context(nc.psum_tensor(f"pGU{u}", [P, 2 * FF], F32)) for u in range(2)]
        pY = [ctx.enter_context(nc.psum_tensor(f"pY{u}", [P, 512], F32)) for u in range(2)]
        src_loaded = [sem(f"src_loaded{r}") for r in range(GI)]
        dst_loaded = [sem(f"dst_loaded{r}") for r in range(GI)]
        gathered = [sem(f"gathered{r}") for r in range(GI)]
        scattered = [sem(f"scattered{r}") for r in range(GI)]
        passed = sem("passed")
        xT_done = sem("xgT_done")
        xT_copied = sem("xgT_copied")
        gu_done = sem("gu_done")
        gate_done = sem("gate_done")
        hid_done = sem("hid_done")
        hidT_done = sem("hidT_done")
        hidT_copied = sem("hidT_copied")
        y_done = sem("y_done")
        y_copied = sem("y_copied")
        block = ctx.enter_context(nc.Block())

        def every_tile(eng, step):
            for n in range(GI):
                step(n, n, 0)
            with eng.Fori(0, SLOT_TILES // GI - 2) as i:
                for r in range(GI):
                    step(GI * i + GI + r, r, i + 1)
            for r in range(GI):
                step(SLOT_TILES - GI + r, r, SLOT_TILES // GI - 1)

        def below(n, k):
            return isinstance(n, int) and n < k

        def last_ones(n, k):
            return isinstance(n, int) and n >= SLOT_TILES - k

        @block.sync
        def _(sp):
            def load(ring, loaded, n, r):
                sp.dma_start(ring[r][:, :], slot_d[bass.ds(n * P, P), :]).then_inc(loaded[r], 16)

            for n in range(GI):
                load(src, src_loaded, n, n)
                load(dst, dst_loaded, n, n)

            def step(n, r, k):
                if not last_ones(n, GI):
                    sp.wait_ge(gathered[r], 16 * (k + 1))
                    load(src, src_loaded, n + GI, r)
                    sp.wait_ge(scattered[r], 16 * (k + 1))
                    load(dst, dst_loaded, n + GI, r)

            every_tile(sp, step)

        @block.gpsimd
        def _(pool):
            def gather(n, r, k):
                pool.wait_ge(src_loaded[r], 16 * (k + 1))
                if not below(n, GI):
                    wait_alone(pool, xT_done, n - GI + 1, passed)
                nc.gpsimd.indirect_dma_start(xg[r][:, :], None, xn_d,
                                             bass.IndirectOffsetOnAxis(src[r][:, 0:1].bitcast(U32), 0),
                                             bounds_check=TOK - 1).then_inc(gathered[r], 16)

            gather(0, 0, 0)
            gather(1, 1, 0)

            def scatter(n, r, k):
                pool.wait_ge(y_copied, n + 1)
                wait_alone(pool, dst_loaded[r], 16 * (k + 1), passed)
                nc.gpsimd.indirect_dma_start(y_d, bass.IndirectOffsetOnAxis(dst[r][:, 1:2].bitcast(U32), 0),
                                             y[r][:, :], None, bounds_check=2 * TOK - 1,
                                             oob_is_err=False).then_inc(scattered[r], 16)

            def step(n, r, k):
                if not last_ones(n, 2):
                    gather(n + 2, (r + 2) % GI, k + (r + 2) // GI)
                if not below(n, 2):
                    scatter(n - 2, (r - 2) % GI, k + (r - 2) // GI)

            every_tile(pool, step)
            for n in range(SLOT_TILES - 2, SLOT_TILES):
                scatter(n, n % GI, n // GI)
            for r in range(GI):
                pool.wait_ge(scattered[r], 16 * SLOT_TILES // GI)

        @block.scalar
        def _(act):
            def step(n, r, k):
                u = r % 2
                act.wait_ge(xT_done, n + 1)
                if not below(n, 2):
                    act.wait_ge(gu_done, n - 1)
                nc.scalar.activation(xgT[u][:, :, :], pXT[:, :, :], ACT.Copy).then_inc(xT_copied, 1)
                act.wait_ge(gu_done, n + 1)
                if not below(n, 2):
                    act.wait_ge(hid_done, n - 1)
                nc.scalar.activation(gate[u][:, :], pGU[u][:, 0:FF], ACT.Silu).then_inc(gate_done, 1)
                if not below(n, 1):
                    y_copy(n - 1, (r - 1) % GI, k + (r - 1) // GI)

            def y_copy(n, r, k):
                act.wait_ge(y_done, n + 1)
                if not below(n, GI):
                    act.wait_ge(scattered[r], 16 * k)
                nc.scalar.activation(y[r][:, :], pY[r % 2][:, 0:D], ACT.Copy).then_inc(y_copied, 1)

            every_tile(act, step)
            y_copy(SLOT_TILES - 1, GI - 1, SLOT_TILES // GI - 1)

        @block.vector
        def _(dve):
            def step(n, r, k):
                u = r % 2
                dve.wait_ge(gate_done, n + 1)
                if not below(n, 2):
                    dve.wait_ge(hidT_done, n - 1)
                nc.vector.tensor_tensor(hid[u][:, :], pGU[u][:, FF:2 * FF], gate[u][:, :], ALU.mult).then_inc(hid_done, 1)
                dve.wait_ge(hidT_done, n + 1)
                if not below(n, 2):
                    dve.wait_ge(y_done, n - 1)
                nc.vector.tensor_copy(hidT[u][:, :, :], pHT[:, :, :]).then_inc(hidT_copied, 1)

            every_tile(dve, step)

        @block.tensor
        def _(pe):
            def transpose_x(n, r, k):
                pe.wait_ge(gathered[r], 16 * (k + 1))
                if not below(n, 1):
                    pe.wait_ge(xT_copied, n)
                for c in range(KC):
                    last = nc.tensor.transpose(pXT[:, c, :], xg[r][:, c * P:(c + 1) * P], ident[:, :])
                last.then_inc(xT_done, 1)

            def gate_up_half(n, u, e, c):
                if c == 0:
                    pe.wait_ge(xT_copied, n + 1)
                    if not below(n, 2):
                        pe.wait_ge(hid_done, n - 1)
                last = nc.tensor.matmul(pGU[u][:, :], xgT[u][:, c, :], w_gu[:, c, bass.ds(e * (2 * FF), 2 * FF)],
                                        start=c == 0, stop=c == KC - 1)
                if c == KC - 1:
                    last.then_inc(gu_done, 1)

            def transpose_h(n, u):
                pe.wait_ge(hid_done, n + 1)
                if not below(n, 1):
                    pe.wait_ge(hidT_copied, n)
                for c in range(KC):
                    last = nc.tensor.transpose(pHT[:, c, :], hid[u][:, c * P:(c + 1) * P], ident[:, :])
                last.then_inc(hidT_done, 1)

            def down_product(n, u, e):
                pe.wait_ge(hidT_copied, n + 1)
                if not below(n, 2):
                    pe.wait_ge(y_copied, n - 1)
                for c in range(KC):
                    last = nc.tensor.matmul(pY[u][:, 0:D], hidT[u][:, c, :], w_dn[:, c, bass.ds(e * D, D)],
                                            start=c == 0, stop=c == KC - 1)
                last.then_inc(y_done, 1)

            def expert_of(n):
                return nc.tensor.value_load(tile_expert[0:1, bass.ds(n, 1)], min_val=0, max_val=EXPERTS - 1)

            transpose_x(0, 0, 0)

            def step(n, r, k):
                u = r % 2
                e = expert_of(n)
                gate_up_half(n, u, e, 0)
                if not below(n, 1):
                    transpose_h(n - 1, 1 - u)
                gate_up_half(n, u, e, 1)
                if not last_ones(n, 1):
                    transpose_x(n + 1, (r + 1) % GI, k + (r + 1) // GI)
                if not below(n, 1):
                    down_product(n - 1, 1 - u, expert_of(n - 1))

            every_tile(pe, step)
            transpose_h(SLOT_TILES - 1, 1)
            down_product(SLOT_TILES - 1, 1, expert_of(SLOT_TILES - 1))


def combine(nc, y_d, weights, acc, out):
    RB = 4
    y_t = y_d.rearrange("(r n j p) d -> r n p j d", r=2, j=JT, p=P)
    out_t = out.rearrange("b (n j p) d -> (b n) p j d", j=JT, p=P)
    with ExitStack() as ctx:
        def sem(name):
            return ctx.enter_context(nc.semaphore(name))

        ys = [[ctx.enter_context(nc.sbuf_tensor(f"ys{q}_{r}", [P, JT, D], F32)) for r in range(2)] for q in range(RB)]
        y_loaded = [sem(f"y_loaded{q}") for q in range(RB)]
        first_added = sem("first_added")
        added = sem("added")
        stored = sem("stored")
        block = ctx.enter_context(nc.Block())

        def every_block(eng, step):
            for n in range(RB):
                step(n, n, 0)
            with eng.Fori(0, NBLK // RB - 1) as i:
                for q in range(RB):
                    step(RB * i + RB + q, q, i + 1)

        @block.sync
        def _(sp):
            def step(n, q, k):
                if not isinstance(n, int):
                    sp.wait_ge(added, n - RB + 1)
                for r in range(2):
                    sp.dma_start(ys[q][r][:, :, :], y_t[r, bass.ds(n, 1)].squeeze(0)).then_inc(y_loaded[q], 16)

            every_block(sp, step)

        @block.vector
        def _(dve):
            def step(n, q, k):
                dve.wait_ge(y_loaded[q], 32 * (k + 1))
                for r in range(2):
                    for j in range(JT):
                        tile = acc[:, bass.ds(n * JT + j, 1), :].squeeze(1)
                        last = nc.vector.scalar_tensor_tensor(tile, ys[q][r][:, j, :],
                                                              weights[:, r, bass.ds(n * JT + j, 1)], tile,
                                                              ALU.mult, ALU.add)
                    if r == 0:
                        last.then_inc(first_added, 1)
                        dve.wait_ge(first_added, n + 1)
                last.then_inc(added, 1)

            every_block(dve, step)

        @block.scalar
        def _(act):
            def step(n, q, k):
                act.wait_ge(added, n + 1)
                act.dma_start(out_t[bass.ds(n, 1)].squeeze(0), acc[:, bass.ds(n * JT, JT), :]).then_inc(stored, 16)

            every_block(act, step)
            act.wait_ge(stored, 16 * NBLK)


def program(nc, x, w_qkv, w_o, gate_w, gate_up, down, out):
    xn_d = nc.dram_tensor("xn_d", (TOK, D), F32, kind="Internal").ap()
    split_d = nc.dram_tensor("split_d", (3, 2, HEADS * HD, TOK), BF16, kind="Internal").ap()
    v_d = nc.dram_tensor("v_d", (HGS, P, TOK // P, GH * VW), F32, kind="Internal").ap()
    o_d = nc.dram_tensor("o_d", (TOK, HEADS * HD), F32, kind="Internal").ap()
    slot_d = nc.dram_tensor("slot_d", (SLOT_TILES * P, 2), I32, kind="Internal").ap()
    y_d = nc.dram_tensor("y_d", (2 * TOK, D), F32, kind="Internal").ap()
    with ExitStack() as ctx:
        def sb(name, shape, dt=F32):
            return ctx.enter_context(nc.sbuf_tensor(name, shape, dt))

        ident = sb("ident", [P, P])
        weights = sb("weights", [P, 2, TOK // P])
        tile_expert = sb("tile_expert", [1, SLOT_TILES], I32)
        w_o_sb = sb("w_o_sb", [P, KC, D])
        w_gu = sb("w_gu", [P, KC, EXPERTS * 2 * FF])
        w_dn = sb("w_dn", [P, KC, EXPERTS * D])
        with ExitStack() as upto_attention:
            def sb1(name, shape, dt=F32):
                return upto_attention.enter_context(nc.sbuf_tensor(name, shape, dt))

            slots = sb1("slots", [P, TOK // P, 2], I32)
            tokens = sb1("tokens", [P, TOK // P, 2, 2], I32)
            with nc.sbuf_tensor("logits", [P, TOK // P, EXPERTS], F32) as logits:
                layernorm_qkv(nc, x, w_qkv, gate_w, xn_d, split_d, v_d, logits, ident)
                route(nc, logits, weights, slots, tokens, tile_expert, slot_d)
            attention(nc, split_d, v_d, o_d, ident, slots, tokens, slot_d,
                      [(w_o_sb, w_o), (w_gu, gate_up), (w_dn, down)])
        with nc.sbuf_tensor("acc", [P, TOK // P, D], F32) as acc:
            project(nc, x, o_d, w_o_sb, acc, ident)
            experts(nc, xn_d, slot_d, tile_expert, w_gu, w_dn, y_d, ident)
            combine(nc, y_d, weights, acc, out)


_INS = ["L0_attn_x", "L0_attn_w_qkv", "L0_attn_w_o", "L0_ffn_gate_w", "L0_ffn_gate_up_proj", "L0_ffn_down_proj"]


def kernel(**inputs):
    import numpy as np
    import concourse.bacc as bacc
    from concourse import mybir as mb
    from concourse.bass_utils import run_bass_kernel_spmd as run

    nc = bacc.Bacc("TRN2", target_bir_lowering=False, num_devices=1)
    arrays, args = {}, []
    for name in _INS:
        a = np.ascontiguousarray(inputs[name])
        arrays[f"in_{name}"] = a
        args.append(nc.dram_tensor(f"in_{name}", a.shape, mb.dt.from_np(a.dtype), kind="ExternalInput").ap())
    out = nc.dram_tensor("out_dram", (BATCH, T, D), F32, kind="ExternalOutput").ap()
    program(nc, *args, out)
    return run(nc, [arrays], core_ids=[0]).results[0]["out_dram"]
```

```python
import concourse.bass as bass
from concourse import mybir
from contextlib import ExitStack

F32 = mybir.dt.float32
BF16 = mybir.dt.bfloat16
I32 = mybir.dt.int32
U32 = mybir.dt.uint32
ALU = mybir.AluOpType
ACT = mybir.ActivationFunctionType
AX = mybir.AxisListType


def wait_alone(eng, sem, value, passed):
    eng.wait_ge(sem, value)
    eng.sem_inc(passed, 1)


BATCH, T, D = 4, 2048, 256
HEADS, HD = 16, 16
TOK = BATCH * T
P = 128
KC = D // P
EXPERTS, FF = 8, 256
LN_EPS = 1e-5
ROUTE_EPS = 1e-9
NEG = -1e30
SCALE = 1.0 / 16.0

BLK = 512
JT = BLK // P
NBLK = TOK // BLK

SLOT_TILES = -(-(2 * TOK + EXPERTS * (P - 1)) // P)
SLOT_TILES += -SLOT_TILES % 8

GH = 4
HGS = HEADS // GH
GROUPS = BATCH * HGS
CH = 512
NCH = T // CH
QT = CH // P
VW = 32
Q_TERMS = [0, 0, 1, 1, 0, 2]
K_TERMS = [0, 1, 0, 1, 2, 0]
QK_ROWS = HD * len(Q_TERMS)
SHIFT_ROWS = 3
B_ROWS = QK_ROWS + SHIFT_ROWS

STEPS = [(c, kt) for c in range(NCH) for kt in range(QT * (c + 1))]
NSTEP = len(STEPS)
LAG = 2
RING = 4


def max_units():
    out = []
    for c in range(NCH):
        for r in range(QT):
            qt = QT * c + r
            for slot in range(c):
                out += [(c, slot, qt, [h], slot * CH, CH, False) for h in range(GH)]
            w = (r + 1) * P
            per = {1: 4, 2: 2, 3: 1, 4: 1}[r + 1]
            out += [(c, c, qt, list(range(h, h + per)), c * CH, w, True) for h in range(0, GH, per)]
    return out


UNITS = max_units()
NUNIT = len(UNITS)


def timetable(lead=74, shift_after=2):
    at = [[] for _ in range(NSTEP)]
    ends, done = [], 0
    for c, kt in STEPS:
        done += CH - P * max(0, kt - QT * c)
        ends.append(done)
    total = ends[-1]

    def put(t, kind, n):
        at[t % NSTEP].append((kind, -(t // NSTEP), n))

    work, last = 0, {}
    for n, (c, slot, qt, heads, k0, w, diag) in enumerate(UNITS):
        work += len(heads) * w // GH
        t = next(x for x in range(-NSTEP, NSTEP)
                 if ends[x % NSTEP] + total * (x // NSTEP) + lead * P >= work)
        put(t, "unit", n)
        last[c] = t
    for c in range(NCH):
        put(last[c], "fold", c)
        put(last[c] + shift_after, "shift", c)
        put(max(s for s, (x, _) in enumerate(STEPS) if x == c) + LAG, "evac", c)
    for row in at:
        row.sort(key=lambda x: (["unit", "fold", "evac", "shift"].index(x[0]), x[1], x[2]))
    return at


TABLE = timetable()
PM_RING = 3
IN_RING = ("unit", "shift")
RING_FIRST = sum(kind in IN_RING and rel == 1 for row in TABLE for kind, rel, n in row)
RING_PERIOD = sum(kind in IN_RING for row in TABLE for kind, rel, n in row)
assert RING_PERIOD % PM_RING == 0


def layernorm_qkv(nc, x, w_qkv, gate_w, xn_d, split_d, v_d, logits, ident):
    x_t = x.rearrange("b (n j p) d -> (b n) p j d", j=JT, p=P)
    xn_t = xn_d.rearrange("(n j p) d -> n p j d", j=JT, p=P)
    with ExitStack() as ctx:
        def sb(name, shape, dt=F32):
            return ctx.enter_context(nc.sbuf_tensor(name, shape, dt))

        def sem(name):
            return ctx.enter_context(nc.semaphore(name))

        w_raw = sb("w_raw", [P, KC, 3 * D])
        w_qk = sb("w_qk", [P, KC, 2, D])
        w_vg = sb("w_vg", [P, KC, D + EXPERTS])
        g_raw = sb("g_raw", [EXPERTS, D])
        x_sb = [sb(f"x_sb{u}", [P, JT, D]) for u in range(2)]
        xn_sb = [sb(f"xn_sb{u}", [P, JT, D]) for u in range(2)]
        xT = [sb(f"xT{u}", [P, KC, BLK]) for u in range(2)]
        stats = sb("stats", [P, JT, 6])
        mv = sb("mv", [P, JT, 2])
        veps = sb("veps", [P, JT])
        std = sb("std", [P, JT])
        inv = sb("inv", [P, JT])
        nwt = sb("nwt", [P, JT])
        nwt2 = sb("nwt2", [P, JT])
        rstd = sb("rstd", [P, JT])
        rest = sb("rest", [P, 4, BLK])
        parts = [sb(f"parts{u}", [P, 4, 3, BLK], BF16) for u in range(2)]
        v_sb = [sb(f"v_sb{u}", [P, HGS, JT, GH * VW]) for u in range(2)]
        pT = ctx.enter_context(nc.psum_tensor("pT", [P, KC, BLK], F32))
        pQK = [ctx.enter_context(nc.psum_tensor(f"pQK{o}", [P, BLK], F32)) for o in range(4)]
        pV = [ctx.enter_context(nc.psum_tensor(f"pV{o}", [P, BLK], F32)) for o in range(2)]

        passed = sem("passed")
        w_loaded = sem("w_loaded")
        w_ready = sem("w_ready")
        ident_zero = sem("ident_zero")
        ident_ready = sem("ident_ready")
        gateT_done = sem("gateT_done")
        gateT_copied = sem("gateT_copied")
        ones_zero = sem("ones_zero")
        v_pad = sem("v_pad")
        x_loaded = [sem(f"x_loaded{u}") for u in range(2)]
        stats_done = sem("stats_done")
        mv_done = sem("mv_done")
        veps_done = sem("veps_done")
        std_done = sem("std_done")
        inv_done = sem("inv_done")
        xn_done = sem("xn_done")
        xT_done = sem("xT_done")
        xT_copied = sem("xT_copied")
        qk_done = sem("qk_done")
        hi_done = sem("hi_done")
        rest_done = sem("rest_done")
        mid_done = sem("mid_done")
        lo_done = sem("lo_done")
        v_done = sem("v_done")
        v_copied = sem("v_copied")
        spilled = [sem(f"spilled{u}") for u in range(2)]
        SPILLS = 16 * 6

        block = ctx.enter_context(nc.Block())

        def every_block(eng, step):
            step(0, 0, 0)
            step(1, 1, 0)
            with eng.Fori(0, NBLK // 2 - 2) as i:
                step(2 * i + 2, 0, i + 1)
                step(2 * i + 3, 1, i + 1)
            step(NBLK - 2, 0, NBLK // 2 - 1)
            step(NBLK - 1, 1, NBLK // 2 - 1)

        def early(n):
            return isinstance(n, int) and n < 2

        def is_block(n, k):
            return isinstance(n, int) and n == k

        @block.sync
        def _(sp):
            sp.dma_start(x_sb[0][:, :, :], x_t[0]).then_inc(x_loaded[0], 16)
            sp.dma_start(w_raw[:, :, :], w_qkv.rearrange("(c p) n -> p c n", p=P)).then_inc(w_loaded, 16)
            sp.dma_start(g_raw[:, :], gate_w).then_inc(w_loaded, 16)
            sp.dma_start(x_sb[1][:, :, :], x_t[1]).then_inc(x_loaded[1], 16)

            def step(n, u, k):
                sp.wait_ge(xn_done, n + 1)
                sp.dma_start(xn_t[bass.ds(n, 1)].squeeze(0), xn_sb[u][:, :, :]).then_inc(spilled[u], 16)
                if not (isinstance(n, int) and n >= NBLK - 2):
                    sp.dma_start(x_sb[u][:, :, :], x_t[bass.ds(n + 2, 1)].squeeze(0)).then_inc(x_loaded[u], 16)
                for o in range(4):
                    side, half = o // 2, o % 2
                    sp.wait_ge(lo_done, 4 * n + o + 1)
                    sp.dma_start(split_d[:, side, half * P:half * P + P, bass.ds(n * BLK, BLK)]
                                 .rearrange("t r c -> r t c"), parts[u][:, o, :, :]).then_inc(spilled[u], 16)
                sp.wait_ge(v_copied, 4 * n + 4)
                sp.dma_start(v_d[:, :, bass.ds(n * JT, JT), :].rearrange("g p j w -> p g j w"),
                             v_sb[u][:, :, :, :]).then_inc(spilled[u], 16)

            every_block(sp, step)
            for u in range(2):
                sp.wait_ge(spilled[u], SPILLS * NBLK // 2)

        @block.gpsimd
        def _(pool):
            nc.gpsimd.memset(ident[:, :], 0.0).then_inc(ident_zero, 1)
            pool.wait_ge(ident_zero, 1)
            nc.gpsimd.affine_select(out=ident[:, :], in_=ident[:, :], compare_op=ALU.not_equal, fill=1.0,
                                    base=0, pattern=[[-1, P]], channel_multiplier=1).then_inc(ident_ready, 1)
            pool.wait_ge(w_loaded, 32)
            for c in range(KC):
                cols = w_raw[:, c, :].rearrange("p (h t d) -> p t h d", t=3, d=HD)
                for t in range(2):
                    nc.gpsimd.tensor_copy(w_qk[:, c, t, :].rearrange("p (h d) -> p h d", d=HD), cols[:, t])
                nc.gpsimd.tensor_copy(w_vg[:, c, 0:D].rearrange("p (h d) -> p h d", d=HD),
                                      cols[:, 2]).then_inc(w_ready, 1)
            for u in range(2):
                nc.gpsimd.memset(v_sb[u][:, :, :, :], 0.0).then_inc(ones_zero, 1)
            pool.wait_ge(ones_zero, 2)
            for u in range(2):
                nc.gpsimd.memset(v_sb[u][:, :, :, :].rearrange("p g j (h w) -> p (g j h) w", w=VW)
                                 [:, :, HD:HD + 1], 1.0).then_inc(v_pad, 1)

            def step(n, u, k):
                for o in range(4):
                    pool.wait_ge(mid_done, 4 * n + o + 1)
                    nc.gpsimd.tensor_tensor(parts[u][:, o, 2, :], rest[:, o, :], parts[u][:, o, 1, :],
                                            ALU.subtract).then_inc(lo_done, 1)

            every_block(pool, step)

        @block.vector
        def _(dve):
            dve.wait_ge(gateT_done, 1)
            nc.vector.tensor_copy(w_vg[:, :, D:D + EXPERTS],
                                  pV[0][:, 0:KC * EXPERTS].rearrange("p (c e) -> p c e", c=KC)).then_inc(gateT_copied, 1)

            def norm(n, u, k):
                dve.wait_ge(x_loaded[u], 16 * (k + 1))
                for j in range(JT):
                    last = nc.vector.bn_stats(stats[:, j, :], x_sb[u][:, j, :])
                last.then_inc(stats_done, 1)
                wait_alone(dve, stats_done, n + 1, passed)
                for j in range(JT):
                    last = nc.vector.bn_aggr(mv[:, j, :], stats[:, j, :])
                last.then_inc(mv_done, 1)
                dve.wait_ge(mv_done, n + 1)
                nc.vector.tensor_scalar(veps[:, :], mv[:, :, 1], LN_EPS, None, ALU.add).then_inc(veps_done, 1)
                dve.wait_ge(std_done, n + 1)
                nc.vector.reciprocal(inv[:, :], std[:, :]).then_inc(inv_done, 1)
                dve.wait_ge(inv_done, 4 * n + 1)
                nc.vector.tensor_tensor(nwt[:, :], inv[:, :], inv[:, :], ALU.mult).then_inc(inv_done, 1)
                dve.wait_ge(inv_done, 4 * n + 2)
                nc.vector.scalar_tensor_tensor(nwt2[:, :], nwt[:, :], -0.5, veps[:, :], ALU.mult, ALU.mult).then_inc(inv_done, 1)
                dve.wait_ge(inv_done, 4 * n + 3)
                nc.vector.scalar_tensor_tensor(rstd[:, :], nwt2[:, :], 1.5, inv[:, :], ALU.add, ALU.mult).then_inc(inv_done, 1)
                dve.wait_ge(inv_done, 4 * n + 4)
                if not early(n):
                    dve.wait_ge(spilled[u], SPILLS * k)
                for j in range(JT):
                    last = nc.vector.tensor_scalar(xn_sb[u][:, j, :], x_sb[u][:, j, :], mv[:, j, 0:1],
                                                   rstd[:, j:j + 1], ALU.subtract, ALU.mult)
                last.then_inc(xn_done, 1)

            norm(0, 0, 0)

            def step(n, u, k):
                if not is_block(n, NBLK - 1):
                    norm(n + 1, 1 - u, k + u)
                for o in range(4):
                    dve.wait_ge(hi_done, 4 * n + o + 1)
                    if not is_block(n, 0):
                        dve.wait_ge(lo_done, 4 * n + o - 3)
                    nc.vector.tensor_tensor(rest[:, o, :], pQK[o][:, :], parts[u][:, o, 0, :],
                                            ALU.subtract).then_inc(rest_done, 1)
                    dve.wait_ge(rest_done, 4 * n + o + 1)
                    nc.vector.tensor_copy(parts[u][:, o, 1, :], rest[:, o, :]).then_inc(mid_done, 1)

            every_block(dve, step)

        @block.scalar
        def _(act):
            def root(n):
                act.wait_ge(veps_done, n + 1)
                nc.scalar.activation(std[:, :], veps[:, :], ACT.Sqrt).then_inc(std_done, 1)

            def xT_copy(n, u):
                act.wait_ge(xT_done, n + 1)
                if not early(n):
                    act.wait_ge(v_done, 4 * n - 4)
                for c in range(KC):
                    last = nc.scalar.activation(xT[u][:, c, :], pT[:, c, :], ACT.Copy)
                last.then_inc(xT_copied, 1)

            root(0)
            xT_copy(0, 0)

            def step(n, u, k):
                if not is_block(n, NBLK - 1):
                    root(n + 1)
                if not early(n):
                    act.wait_ge(spilled[u], SPILLS * k)
                for o in range(4):
                    act.wait_ge(qk_done, 4 * n + o + 1)
                    nc.scalar.activation(parts[u][:, o, 0, :], pQK[o][:, :], ACT.Copy).then_inc(hi_done, 1)
                if not is_block(n, NBLK - 1):
                    xT_copy(n + 1, 1 - u)
                if is_block(n, 0):
                    act.wait_ge(v_pad, 2)
                for j in range(JT):
                    act.wait_ge(v_done, 4 * n + j + 1)
                    nc.scalar.activation(
                        v_sb[u][:, :, j, :].rearrange("p g (h w) -> p g h w", w=VW)[:, :, :, 0:HD],
                        pV[j % 2][:, 0:D].rearrange("p (g h d) -> p g h d", g=HGS, d=HD), ACT.Copy)
                    nc.scalar.activation(logits[:, bass.ds(n * JT + j, 1), :].squeeze(1),
                                         pV[j % 2][:, D:D + EXPERTS], ACT.Copy).then_inc(v_copied, 1)

            every_block(act, step)

        @block.tensor
        def _(pe):
            pe.wait_ge(ident_ready, 1)
            pe.wait_ge(w_loaded, 32)
            for c in range(KC):
                last = nc.tensor.transpose(pV[0][:, c * EXPERTS:(c + 1) * EXPERTS], g_raw[:, c * P:(c + 1) * P],
                                           ident[0:EXPERTS, 0:EXPERTS])
            last.then_inc(gateT_done, 1)

            def transposes(n, u):
                pe.wait_ge(xn_done, n + 1)
                if not is_block(n, 0):
                    pe.wait_ge(xT_copied, n)
                for c in range(KC):
                    for j in range(JT):
                        last = nc.tensor.transpose(pT[:, c, j * P:(j + 1) * P], xn_sb[u][:, j, c * P:(c + 1) * P],
                                                   ident[:, :])
                last.then_inc(xT_done, 1)

            transposes(0, 0)
            pe.wait_ge(w_ready, KC)
            pe.wait_ge(gateT_copied, 1)

            def step(n, u, k):
                pe.wait_ge(xT_copied, n + 1)
                for o in range(4):
                    side, half = o // 2, o % 2
                    if not is_block(n, 0):
                        pe.wait_ge(rest_done, 4 * n + o - 3)
                    for c in range(KC):
                        last = nc.tensor.matmul(pQK[o][:, :], w_qk[:, c, side, half * P:half * P + P],
                                                xT[u][:, c, :], start=c == 0, stop=c == KC - 1)
                    last.then_inc(qk_done, 1)
                if not is_block(n, NBLK - 1):
                    transposes(n + 1, 1 - u)
                for j in range(JT):
                    if not (is_block(n, 0) and j < 2):
                        pe.wait_ge(v_copied, 4 * n + j - 1)
                    for c in range(KC):
                        last = nc.tensor.matmul(pV[j % 2][:, 0:D + EXPERTS], xT[u][:, c, j * P:(j + 1) * P],
                                                w_vg[:, c, :], start=c == 0, stop=c == KC - 1)
                    last.then_inc(v_done, 1)

            every_block(pe, step)


OPS = 16 * 2 * len(Q_TERMS)


class FirstOperands:
    def __init__(self, nc, ctx):
        def sb(name, shape, dt=F32):
            return ctx.enter_context(nc.sbuf_tensor(name, shape, dt))

        self.q = sb("q_op0", [B_ROWS, GH, T], BF16)
        self.k = sb("k_op0", [B_ROWS, GH, T], BF16)
        self.v = sb("v_op0", [P, T // P, GH, VW])
        self.ident = sb("ident_b", [P, P], BF16)
        self.mask = sb("mask_b", [P, P], BF16)
        self.qk_loaded = ctx.enter_context(nc.semaphore("op_loaded0"))
        self.v_loaded = ctx.enter_context(nc.semaphore("v_loaded0"))


def load_qk_of(eng, split_d, g, q, k, loaded):
    rows = bass.ds(g % HGS * (GH * HD), GH * HD)
    cols = bass.ds(g // HGS * T, T)
    for side, (op, terms) in enumerate(((q, Q_TERMS), (k, K_TERMS))):
        for t, part in enumerate(terms):
            eng.dma_start(op[t * HD:(t + 1) * HD, :, :],
                          split_d[part, side, rows, cols].rearrange("(h d) c -> d h c", d=HD)).then_inc(loaded, 16)


def load_v_of(eng, v_d, g, v, loaded):
    eng.dma_start(v[:, :, :, :].rearrange("p k h w -> p k (h w)"),
                  v_d[bass.ds(g % HGS, 1), :, bass.ds(g // HGS * (T // P), T // P), :].squeeze(0)
                  ).then_inc(loaded, 16)


def attention(nc, first_ops, split_d, v_d, o_d, sums_d, slots, tokens, slot_d, preload):
    with ExitStack() as ctx:
        def sb(name, shape, dt=F32):
            return ctx.enter_context(nc.sbuf_tensor(name, shape, dt))

        def ps(name, shape, dt=F32):
            return ctx.enter_context(nc.psum_tensor(name, shape, dt))

        def sem(name):
            return ctx.enter_context(nc.semaphore(name))

        q_op = [first_ops.q, sb("q_op1", [B_ROWS, GH, T], BF16)]
        k_op = [first_ops.k, sb("k_op1", [B_ROWS, GH, T], BF16)]
        v_op = [first_ops.v, sb("v_op1", [P, T // P, GH, VW])]
        ident_b, mask_b = first_ops.ident, first_ops.mask
        prob = [sb(f"prob{r}", [P, GH, CH]) for r in range(RING)]
        part_max = [sb(f"part_max{u}", [P, GH, QT, NCH]) for u in range(2)]
        shift = sb("shift", [P, GH * QT])
        shift_r = sb("shift_r", [P, GH * QT])
        shift_r2 = sb("shift_r2", [P, GH * QT])
        shift_p = sb("shift_p", [P, GH, SHIFT_ROWS, QT], BF16)
        shiftT = sb("shiftT", [SHIFT_ROWS * GH * QT, P], BF16)
        oT_sb = [sb(f"oT_sb{u}", [P, CH]) for u in range(2)]
        SENDS = 2 * TOK // P // GROUPS
        slot_now = [sb(f"slot_now{q}", [P, 1], I32) for q in range(SENDS)]
        token_now = [sb(f"token_now{q}", [P, 2], I32) for q in range(SENDS)]
        pS = [ps(f"pS{u}", [P, 2, CH]) for u in range(2)]
        pM = [ps(f"pM{u}", [P, CH]) for u in range(PM_RING)]
        pO = ps("pO", [P, CH])

        passed = sem("passed")
        pe_passed = sem("pe_passed")
        ones_set = sem("ones_set")
        op_loaded = [first_ops.qk_loaded, sem("op_loaded1")]
        v_loaded = [first_ops.v_loaded, sem("v_loaded1")]
        scores_done = sem("scores_done")
        exp_done = sem("exp_done")
        masked = sem("masked")
        pv_done = sem("pv_done")
        ring_written = sem("ring_written")
        ring_read = sem("ring_read")
        shift_max = sem("shift_max")
        shift_step = sem("shift_step")
        shift_loaded = [sem(f"shift_loaded{c}") for c in range(NCH)]
        o_copied = sem("o_copied")
        o_stored = [sem(f"o_stored{u}") for u in range(2)]
        w_preloaded = sem("w_preloaded")
        slot_picked = sem("slot_picked")
        slot_sent = [sem(f"slot_sent{q}") for q in range(SENDS)]
        SHIFTS = 16 * GH
        STORES = 16 * (GH + 1)

        block = ctx.enter_context(nc.Block())

        def every_period(eng, period):
            period(0, 0, 0, "first")
            with eng.Fori(0, GROUPS // 2 - 1) as i:
                period(2 * i + 1, 1, i, "inner")
                period(2 * i + 2, 0, i + 1, "inner")
            period(GROUPS - 1, 1, GROUPS // 2 - 1, "last")

        def items(s, where):
            for kind, rel, n in TABLE[s]:
                if where == "last" and rel > 0 or where == "first" and rel < 0:
                    continue
                yield kind, rel, n

        def before_first():
            return [(kind, n) for row in TABLE for kind, rel, n in row if rel == 1]

        def after_last():
            return [(kind, n) for row in TABLE for kind, rel, n in row if rel == -1]

        def place_in_period(kind, rel, n, where):
            entries = [x for s in range(NSTEP) for x in items(s, where) if x[0] in IN_RING]
            return entries.index((kind, rel, n))

        def in_ring(g, kind, rel, n, where):
            if where == "before":
                x = [y for y in before_first() if y[0] in IN_RING].index((kind, n))
                return x, x % PM_RING
            x = RING_FIRST + place_in_period(kind, rel, n, where)
            return RING_PERIOD * g + x, x % PM_RING

        def shift_before(g, rel, c, where):
            rel, c = (rel, c - 1) if c else (rel - 1, NCH - 1)
            if isinstance(g, int) and g + rel < 0:
                return None
            stands = next(r for row in TABLE for kind, r, n in row if (kind, n) == ("shift", c))
            if rel == stands:
                return in_ring(g, "shift", stands, c, where)[0] + 1
            assert rel == stands - 1
            if isinstance(g, int) and g == 0:
                return in_ring(0, "shift", stands, c, "before")[0] + 1
            return in_ring(g - 1, "shift", stands, c, "inner")[0] + 1

        @block.sync
        def _(sp):
            def load_qk(g, v, wait):
                if wait is not None:
                    sp.wait_ge(scores_done, wait)
                load_qk_of(sp, split_d, g, q_op[v], k_op[v], op_loaded[v])

            def load_v(g, v, wait):
                if wait is not None:
                    sp.wait_ge(pv_done, wait)
                load_v_of(sp, v_d, g, v_op[v], v_loaded[v])

            def send_shift(g, v, c, number):
                sp.wait_ge(ring_read, number + 1)
                for h in range(GH):
                    sp.dma_start(q_op[v][QK_ROWS:B_ROWS, h, c * CH:(c + 1) * CH].rearrange("r (q p) -> r q p", p=P),
                                 shiftT[h * SHIFT_ROWS * QT:(h + 1) * SHIFT_ROWS * QT, :]).then_inc(shift_loaded[c], 16)

            def store(g, c):
                sp.wait_ge(o_copied, NCH * g + c + 1)
                for h in range(GH):
                    sp.dma_start(o_d[bass.ds(g % HGS * GH + h, 1), :, bass.ds(g // HGS * T + c * CH, CH)].squeeze(0),
                                 oT_sb[c % 2][h * VW:h * VW + HD, :]).then_inc(o_stored[c % 2], 16)
                sp.dma_start(sums_d[bass.ds(g % HGS * GH, GH), bass.ds(g // HGS * T + c * CH, CH)],
                             oT_sb[c % 2][HD:P:VW, :]).then_inc(o_stored[c % 2], 16)

            (w_o_sb, w_o), *expert_weights = preload
            sp.dma_start(w_o_sb[:, :, :], w_o.rearrange("(c p) n -> p c n", p=P)).then_inc(w_preloaded, 16)
            for to, w in expert_weights:
                for c in range(KC):
                    sp.dma_start(to[:, c, :].rearrange("p (e n) -> p e n", e=EXPERTS),
                                 w[:, c * P:(c + 1) * P, :].rearrange("e p n -> p e n")).then_inc(w_preloaded, 16)
            for kind, n in before_first():
                if kind == "shift":
                    send_shift(0, 0, n, in_ring(0, kind, 1, n, "before")[0])

            def period(g, u, k, where):
                for s in range(NSTEP):
                    if s == 0 and where != "last":
                        load_qk(g + 1, 1 - u, None if where == "first" else 2 * NSTEP * g)
                    if s == LAG + 1 and where != "last":
                        load_v(g + 1, 1 - u, None if where == "first" else NSTEP * g)
                    for kind, rel, n in items(s, where):
                        if kind == "shift":
                            send_shift(g + rel, (u + rel) % 2, n, in_ring(g, kind, rel, n, where)[0])
                        if kind == "evac":
                            store(g + rel, n)

            every_period(sp, period)
            for kind, n in after_last():
                if kind == "evac":
                    store(GROUPS - 1, n)
            for u in range(2):
                sp.wait_ge(o_stored[u], STORES * GROUPS * NCH // 2)
            sp.wait_ge(w_preloaded, 16 * 5)

        @block.gpsimd
        def _(pool):
            nc.gpsimd.memset(k_op[1][QK_ROWS:B_ROWS, :, :], 1.0).then_inc(ones_set, 1)
            pool.wait_ge(ones_set, 1)

            def byhead(x):
                return x[:, :].rearrange("p (h q) -> p h q", h=GH)

            def split_shift(g, c, transposed):
                at = 5 * (NCH * g + c)
                if transposed is not None:
                    pool.wait_ge(ring_written, transposed)
                wait_alone(pool, shift_max, NCH * g + c + 1, passed)
                nc.gpsimd.tensor_copy(shift_p[:, :, 0, :], byhead(shift)).then_inc(shift_step, 1)
                pool.wait_ge(shift_step, at + 1)
                nc.gpsimd.tensor_tensor(byhead(shift_r), byhead(shift), shift_p[:, :, 0, :], ALU.subtract).then_inc(shift_step, 1)
                wait_alone(pool, shift_step, at + 2, passed)
                nc.gpsimd.tensor_copy(shift_p[:, :, 1, :], byhead(shift_r)).then_inc(shift_step, 1)
                pool.wait_ge(shift_step, at + 3)
                nc.gpsimd.tensor_tensor(byhead(shift_r2), byhead(shift_r), shift_p[:, :, 1, :], ALU.subtract).then_inc(shift_step, 1)
                wait_alone(pool, shift_step, at + 4, passed)
                nc.gpsimd.tensor_copy(shift_p[:, :, 2, :], byhead(shift_r2)).then_inc(shift_step, 1)

            def place(g, q, where):
                tile, rank = g * (SENDS // 2) + q // 2, q % 2
                if where != "first":
                    wait_alone(pool, slot_sent[q], 16 * g, passed)
                nc.gpsimd.tensor_copy(slot_now[q][:, :], slots[:, bass.ds(tile, 1), rank])
                nc.gpsimd.tensor_copy(token_now[q][:, :], tokens[:, bass.ds(tile, 1), rank, :].squeeze(1)).then_inc(slot_picked, 1)
                wait_alone(pool, slot_picked, SENDS * g + q + 1, passed)
                nc.gpsimd.indirect_dma_start(slot_d, bass.IndirectOffsetOnAxis(slot_now[q][:, 0:1].bitcast(U32), 0),
                                             token_now[q][:, :], None,
                                             bounds_check=SLOT_TILES * P - 1).then_inc(slot_sent[q], 16)

            for kind, n in before_first():
                if kind == "fold":
                    split_shift(0, n, shift_before(-1, 1, n, "before"))

            def period(g, u, k, where):
                for s, (c, kt) in enumerate(STEPS):
                    if kt >= QT * c:
                        w0 = (kt - QT * c) * P
                        wait_alone(pool, exp_done, 2 * (NSTEP * g + s) + 2, passed)
                        tri = prob[s % RING][:, :, w0:w0 + P]
                        nc.gpsimd.affine_select(out=tri, in_=tri, compare_op=ALU.is_ge, fill=0.0, base=0,
                                                pattern=[[0, GH], [1, P]], channel_multiplier=-1).then_inc(masked, 1)
                    for kind, rel, n in items(s, where):
                        if kind == "fold":
                            split_shift(g + rel, n, shift_before(g, rel, n, where))
                    if s % 4 == 2 and s // 4 < SENDS:
                        place(g, s // 4, where)

            every_period(pool, period)
            for q in range(SENDS):
                pool.wait_ge(slot_sent[q], 16 * GROUPS)

        @block.vector
        def _(dve):
            def unit(n, number, bank):
                c, slot, qt, heads, k0, w, diag = UNITS[n]
                dve.wait_ge(ring_written, number + 1)
                nc.vector.tensor_reduce(part_max[c % 2][:, heads[0]:heads[-1] + 1, qt % QT, slot:slot + 1],
                                        pM[bank][:, 0:len(heads) * w].rearrange("p (h k) -> p h k", k=w),
                                        AX.X, ALU.max).then_inc(ring_read, 1)

            def fold(g, c, number):
                dve.wait_ge(ring_read, number + 1)
                if not (isinstance(g, int) and g == 0 and c == 0):
                    dve.wait_ge(shift_step, 5 * (NCH * g + c))
                nc.vector.tensor_reduce(shift[:, :].rearrange("p (h q) -> p h q", h=GH),
                                        part_max[c % 2][:, :, :, 0:c + 1], AX.X, ALU.max,
                                        negate=True).then_inc(shift_max, 1)

            def shift_copy(g, c, number, bank):
                dve.wait_ge(ring_written, number + 1)
                if not (isinstance(g, int) and g == 0 and c == 0):
                    before = (g, c - 1) if c else (g - 1, NCH - 1)
                    dve.wait_ge(shift_loaded[before[1]], SHIFTS * (before[0] + 1))
                nc.vector.tensor_copy(shiftT[:, :], pM[bank][0:SHIFT_ROWS * GH * QT, 0:P // 2].bitcast(BF16)
                                      ).then_inc(ring_read, 1)

            def do(g, kind, rel, n, where):
                if kind == "unit":
                    unit(n, *in_ring(g, kind, rel, n, where))
                if kind == "shift":
                    shift_copy(g + rel, n, *in_ring(g, kind, rel, n, where))
                if kind == "fold":
                    last_unit = max(m for m, x in enumerate(UNITS) if x[0] == n)
                    fold(g + rel, n, in_ring(g, "unit", rel, last_unit, where)[0])

            for kind, n in before_first():
                do(-1, kind, 1, n, "before")

            def period(g, u, k, where):
                for s in range(NSTEP):
                    for kind, rel, n in items(s, where):
                        do(g, kind, rel, n, where)

            every_period(dve, period)

        @block.scalar
        def _(act):
            def evac(g, c):
                e = NCH * g + c
                act.wait_ge(pv_done, NSTEP * g + max(s for s, (x, _) in enumerate(STEPS) if x == c) + 1)
                if isinstance(g, int) and g == 0:
                    if c >= 2:
                        act.wait_ge(o_stored[c % 2], STORES * (c // 2))
                else:
                    act.wait_ge(o_stored[c % 2], STORES * (2 * g + c // 2))
                nc.scalar.activation(oT_sb[c % 2][:, :], pO[:, :], ACT.Copy).then_inc(o_copied, 1)

            def period(g, u, k, where):
                for s, (c, kt) in enumerate(STEPS):
                    w0 = P * max(0, kt - QT * c)
                    if not (where == "first" and s < RING):
                        act.wait_ge(pv_done, NSTEP * g + s - RING + 1)
                    for pair in range(2):
                        act.wait_ge(scores_done, 2 * (NSTEP * g + s) + pair + 1)
                        nc.scalar.activation(prob[s % RING][:, 2 * pair:2 * pair + 2, w0:CH],
                                             pS[pair][:, :, w0:CH], ACT.Exp, scale=SCALE).then_inc(exp_done, 1)
                    for kind, rel, n in items(s, where):
                        if kind == "evac":
                            evac(g + rel, n)

            every_period(act, period)
            for kind, n in after_last():
                if kind == "evac":
                    evac(GROUPS - 1, n)

        @block.tensor
        def _(pe):

            def ring_free(number):
                if not (isinstance(number, int) and number < PM_RING):
                    pe.wait_ge(ring_read, number - PM_RING + 1)

            def unit(v, kv, n, number, bank):
                c, slot, qt, heads, k0, w, diag = UNITS[n]
                if n == 0:
                    pe.wait_ge(op_loaded[v], OPS * (kv + 1))
                ring_free(number)
                for x, h in enumerate(heads):
                    last = nc.tensor.matmul(pM[bank][:, x * w:(x + 1) * w], q_op[v][0:QK_ROWS, h, qt * P:(qt + 1) * P],
                                            k_op[v][0:QK_ROWS, h, k0:k0 + w], start=True, stop=not diag)
                    if diag:
                        last = nc.tensor.matmul(pM[bank][:, (x + 1) * w - P:(x + 1) * w], ident_b[:, :], mask_b[:, :],
                                                start=False, stop=True)
                last.then_inc(ring_written, 1)

            def shift_transpose(g, c, number, bank):
                ring_free(number)
                wait_alone(pe, shift_step, 5 * (NCH * g + c) + 5, pe_passed)
                nc.tensor.transpose(pM[bank][0:SHIFT_ROWS * GH * QT, 0:P // 2].bitcast(BF16),
                                    shift_p[:, :, :, :].rearrange("p h r q -> p (h r q)"),
                                    ident_b[:, :]).then_inc(ring_written, 1)

            def scores(g, u, s, pair, where):
                c, kt = STEPS[s]
                w0 = P * max(0, kt - QT * c)
                if s == 0 and pair == 0 and u == 1 and where != "last":
                    pe.wait_ge(ones_set, 1)
                if kt == 0 and pair == 0:
                    pe.wait_ge(shift_loaded[c], SHIFTS * (g + 1))
                if not (where == "first" and s == 0):
                    pe.wait_ge(exp_done, 2 * (NSTEP * g + s) + pair - 1)
                for x in range(2):
                    h = 2 * pair + x
                    last = nc.tensor.matmul(pS[pair][:, x, w0:CH], k_op[u][:, h, kt * P:(kt + 1) * P],
                                            q_op[u][:, h, c * CH + w0:(c + 1) * CH], start=True, stop=True)
                last.then_inc(scores_done, 1)

            def values(g, u, k, s):
                c, kt = STEPS[s]
                w0 = P * max(0, kt - QT * c)
                if s == 0:
                    pe.wait_ge(v_loaded[u], 16 * (k + 1))
                if kt >= QT * c:
                    pe.wait_ge(masked, NCH * QT * g + kt + 1)
                else:
                    pe.wait_ge(exp_done, 2 * (NSTEP * g + s) + 2)
                if kt == 0 and not (isinstance(g, int) and g == 0 and c == 0):
                    pe.wait_ge(o_copied, NCH * g + c)
                for h in range(GH):
                    last = nc.tensor.matmul(pO[h * VW:(h + 1) * VW, w0:CH], v_op[u][:, kt, h, :],
                                            prob[s % RING][:, h, w0:CH], start=kt == 0, stop=kt == QT * (c + 1) - 1,
                                            tile_position=(0, h * VW))
                last.then_inc(pv_done, 1)

            for kind, n in before_first():
                if kind in IN_RING:
                    number, bank = in_ring(0, kind, 1, n, "before")
                    unit(0, 0, n, number, bank) if kind == "unit" else shift_transpose(0, n, number, bank)

            def period(g, u, k, where):
                for s in range(NSTEP):
                    todo = [(rel, n) for kind, rel, n in items(s, where) if kind == "unit"]
                    for slot in range(4):
                        for rel, n in todo[len(todo) * slot // 4:len(todo) * (slot + 1) // 4]:
                            unit((u + rel) % 2, k + (u if rel else 0), n, *in_ring(g, "unit", rel, n, where))
                        if slot < 2:
                            scores(g, u, s, slot, where)
                        elif slot == 2 and s >= LAG:
                            values(g, u, k, s - LAG)
                        elif slot == 2 and where != "first":
                            values(g - 1, 1 - u, k - (1 - u), NSTEP + s - LAG)
                    for kind, rel, n in items(s, where):
                        if kind == "shift":
                            shift_transpose(g + rel, n, *in_ring(g, kind, rel, n, where))

            every_period(pe, period)
            for s in range(NSTEP - LAG, NSTEP):
                values(GROUPS - 1, 1, GROUPS // 2 - 1, s)


def route(nc, logits, weights, slots, tokens, tile_expert, slot_d, first_ops, split_d, v_d):
    NT = TOK // P
    with ExitStack() as ctx:
        def sb(name, shape, dt=F32):
            return ctx.enter_context(nc.sbuf_tensor(name, shape, dt))

        def sem(name):
            return ctx.enter_context(nc.semaphore(name))

        full = [P, NT, EXPERTS]
        e_int = sb("e_int", full, I32)
        e_less = sb("e_less", full)
        z = sb("z", full)
        ez = sb("ez", full)
        prb = sb("prb", full)
        eq = sb("eq", full)
        cand = sb("cand", full)
        hot = [sb(f"hot{r}", full) for r in range(2)]
        best = [sb(f"best{r}", [P, NT]) for r in range(2)]
        first = sb("first", [P, NT])
        mx = sb("mx", [P, NT])
        total = sb("total", [P, NT])
        inv = sb("inv_total", [P, NT])
        tk = [sb(f"tk{r}", [P, NT]) for r in range(2)]
        sel = sb("sel", full)
        zero = sb("zero", [P, NT])
        cum = sb("cum", [P, EXPERTS, NT])
        tiles_i = sb("tiles_i", [P, EXPERTS], I32)
        tiles_i2 = sb("tiles_i2", [P, EXPERTS], I32)
        tiles_f = sb("tiles_f", [P, EXPERTS])
        ends = sb("ends", [P, EXPERTS])
        begins = sb("begins", [P, EXPERTS])
        pos = sb("pos", full)
        slot_f = sb("slot_f", [P, NT])
        lower = sb("lower", [P, P])
        ones = sb("ones", [P, P])
        pad = sb("pad", [P, SLOT_TILES, 2], I32)
        j_int = sb("j_int", [1, SLOT_TILES, EXPERTS], I32)
        j_f = sb("j_f", [1, SLOT_TILES, EXPERTS])
        j_ge = sb("j_ge", [1, SLOT_TILES, EXPERTS])
        j_e = sb("j_e", [1, SLOT_TILES])
        pBefore = ctx.enter_context(nc.psum_tensor("pBefore", full, F32))
        pTile = ctx.enter_context(nc.psum_tensor("pTile", full, F32))

        made = sem("made")
        consts = sem("consts")
        consts_b = sem("consts_b")
        filled = sem("filled")
        chain = sem("chain")
        z_done = sem("z_done")
        ez_done = sem("ez_done")
        sel_done = sem("sel_done")
        counted = sem("counted")
        pad_sent = sem("pad_sent")
        block = ctx.enter_context(nc.Block())

        def over_experts(x):
            return x[:, :].unsqueeze(2).to_broadcast(full)

        @block.gpsimd
        def _(pool):
            nc.gpsimd.iota(e_int[:, :, :], [[0, NT], [1, EXPERTS]], base=-EXPERTS, channel_multiplier=0).then_inc(made, 1)
            nc.gpsimd.iota(j_int[:, :, :], [[1, SLOT_TILES], [0, EXPERTS]], base=0, channel_multiplier=0).then_inc(made, 1)
            nc.gpsimd.memset(ones[:, :], 1.0).then_inc(made, 1)
            nc.gpsimd.memset(lower[:, :], 1.0).then_inc(made, 1)
            nc.gpsimd.memset(zero[:, :], 0.0).then_inc(made, 1)
            nc.gpsimd.iota(tokens[:, :, :, 0], [[P, NT], [0, 2]], base=0, channel_multiplier=1).then_inc(made, 1)
            nc.gpsimd.iota(tokens[:, :, :, 1], [[P, NT], [TOK, 2]], base=0, channel_multiplier=1).then_inc(made, 1)
            nc.gpsimd.iota(pad[:, :, :], [[0, SLOT_TILES], [2 * TOK, 2]], base=0, channel_multiplier=0).then_inc(made, 1)
            pool.wait_ge(made, 4)
            nc.gpsimd.affine_select(out=lower[:, :], in_=lower[:, :], compare_op=ALU.is_gt, fill=0.0, base=0,
                                    pattern=[[1, P]], channel_multiplier=-1).then_inc(filled, 1)
            ident_b, mask_b = first_ops.ident, first_ops.mask
            nc.gpsimd.memset(ident_b[:, :], 0.0).then_inc(consts, 1)
            nc.gpsimd.memset(mask_b[:, :], 0.0).then_inc(consts, 1)
            pool.wait_ge(consts, 2)
            nc.gpsimd.affine_select(out=ident_b[:, :], in_=ident_b[:, :], compare_op=ALU.not_equal, fill=1.0,
                                    base=0, pattern=[[-1, P]], channel_multiplier=1).then_inc(consts_b, 1)
            nc.gpsimd.affine_select(out=mask_b[:, :], in_=mask_b[:, :], compare_op=ALU.is_ge, fill=NEG,
                                    base=0, pattern=[[-1, P]], channel_multiplier=1).then_inc(consts_b, 1)
            pool.wait_ge(consts_b, 2)
            nc.gpsimd.memset(first_ops.k[QK_ROWS:B_ROWS, :, :], 1.0).then_inc(consts_b, 1)

        @block.sync
        def _(sp):
            load_qk_of(sp, split_d, 0, first_ops.q, first_ops.k, first_ops.qk_loaded)
            load_v_of(sp, v_d, 0, first_ops.v, first_ops.v_loaded)
            sp.wait_ge(consts_b, 3)
            sp.wait_ge(made, 8)
            sp.dma_start(slot_d.rearrange("(p n) c -> p (n c)", p=P),
                         pad[:, :, :].rearrange("p n c -> p (n c)")).then_inc(pad_sent, 16)
            sp.wait_ge(pad_sent, 16)

        @block.scalar
        def _(act):
            act.wait_ge(z_done, 1)
            nc.scalar.activation(ez[:, :, :], z[:, :, :], ACT.Exp).then_inc(ez_done, 1)

        @block.tensor
        def _(pe):
            pe.wait_ge(filled, 1)
            pe.wait_ge(made, 8)
            pe.wait_ge(sel_done, 1)
            for out, lhsT in ((pBefore, lower), (pTile, ones)):
                nc.tensor.matmul(out[:, :, :].rearrange("p t e -> p (t e)"), lhsT[:, :],
                                 sel[:, :, :].rearrange("p t e -> p (t e)"), start=True, stop=True).then_inc(counted, 1)

        @block.vector
        def _(dve):
            done = [0]

            def link(ins):
                done[0] += 1
                ins.then_inc(chain, 1)
                dve.wait_ge(chain, done[0])

            V = nc.vector
            dve.wait_ge(made, 8)
            link(V.tensor_copy(e_less[:, :, :], e_int[:, :, :]))
            link(V.tensor_reduce(mx[:, :], logits[:, :, :], AX.X, ALU.max))
            V.tensor_tensor(z[:, :, :], logits[:, :, :], over_experts(mx), ALU.subtract).then_inc(z_done, 1)
            dve.wait_ge(ez_done, 1)
            link(V.tensor_reduce(total[:, :], ez[:, :, :], AX.X, ALU.add))
            link(V.reciprocal(inv[:, :], total[:, :]))
            link(V.tensor_tensor(prb[:, :, :], ez[:, :, :], over_experts(inv), ALU.mult))
            for r in range(2):
                link(V.tensor_reduce(best[r][:, :], prb[:, :, :], AX.X, ALU.max))
                link(V.tensor_tensor(eq[:, :, :], prb[:, :, :], over_experts(best[r]), ALU.is_equal))
                link(V.tensor_tensor(cand[:, :, :], eq[:, :, :], e_less[:, :, :], ALU.mult))
                link(V.tensor_reduce(first[:, :], cand[:, :, :], AX.X, ALU.min))
                link(V.tensor_tensor(hot[r][:, :, :], e_less[:, :, :], over_experts(first), ALU.is_equal))
                if r == 0:
                    link(V.scalar_tensor_tensor(prb[:, :, :], hot[0][:, :, :], -2.0, prb[:, :, :], ALU.mult, ALU.add))
            V.tensor_tensor(sel[:, :, :], hot[0][:, :, :], hot[1][:, :, :], ALU.add).then_inc(sel_done, 1)
            link(V.tensor_tensor(total[:, :], best[0][:, :], best[1][:, :], ALU.add))
            link(V.tensor_scalar(total[:, :], total[:, :], ROUTE_EPS, None, ALU.add))
            link(V.reciprocal(inv[:, :], total[:, :]))
            for r in range(2):
                link(V.tensor_tensor(tk[r][:, :], best[r][:, :], inv[:, :], ALU.mult))
            link(V.tensor_tensor(total[:, :], tk[0][:, :], tk[1][:, :], ALU.add))
            link(V.tensor_scalar(total[:, :], total[:, :], ROUTE_EPS, None, ALU.add))
            link(V.reciprocal(inv[:, :], total[:, :]))
            for r in range(2):
                link(V.tensor_tensor(weights[:, r, :], tk[r][:, :], inv[:, :], ALU.mult))
            dve.wait_ge(counted, 2)
            for e in range(EXPERTS):
                link(V.tensor_tensor_scan(cum[:, e, :], pTile[:, :, e], zero[:, :], 0.0, ALU.add, ALU.add))
            link(V.tensor_scalar(tiles_i[:, :], cum[:, :, NT - 1], float(P - 1), None, ALU.add))
            link(V.tensor_scalar(tiles_i2[:, :], tiles_i[:, :], 7, None, ALU.logical_shift_right))
            link(V.tensor_copy(tiles_f[:, :], tiles_i2[:, :]))
            link(V.tensor_tensor_scan(ends[:, :], tiles_f[:, :], zero[:, 0:EXPERTS], 0.0, ALU.add, ALU.add))
            link(V.tensor_tensor(begins[:, :], ends[:, :], tiles_f[:, :], ALU.subtract))
            link(V.tensor_scalar(begins[:, :], begins[:, :], float(P), None, ALU.mult))
            link(V.tensor_tensor(pos[:, :, :], cum[:, :, :].rearrange("p e t -> p t e"), pTile[:, :, :], ALU.subtract))
            link(V.tensor_tensor(pos[:, :, :], pos[:, :, :], pBefore[:, :, :], ALU.add))
            link(V.tensor_tensor(pos[:, :, :], pos[:, :, :], begins[:, :].unsqueeze(1).to_broadcast(full), ALU.add))
            for r in range(2):
                link(V.tensor_tensor(cand[:, :, :], pos[:, :, :], hot[r][:, :, :], ALU.mult))
                link(V.tensor_reduce(slot_f[:, :], cand[:, :, :], AX.X, ALU.add))
                link(V.tensor_copy(slots[:, :, r], slot_f[:, :]))
            link(V.tensor_copy(j_f[:, :, :], j_int[:, :, :]))
            link(V.tensor_tensor(j_ge[:, :, :], j_f[:, :, :],
                                 ends[0:1, :].unsqueeze(1).to_broadcast([1, SLOT_TILES, EXPERTS]), ALU.is_ge))
            link(V.tensor_reduce(j_e[:, :], j_ge[:, :, :], AX.X, ALU.add))
            link(V.tensor_scalar(j_e[:, :], j_e[:, :], float(EXPERTS - 1), None, ALU.min))
            link(V.tensor_copy(tile_expert[:, :], j_e[:, :]))


def experts(nc, xn_d, slot_d, tile_expert, w_gu, w_dn, y_d, ident, x, o_d, sums_d, inv_d, w_o_sb, acc):
    x_t = x.rearrange("b (n j p) d -> (b n) p j d", j=JT, p=P)
    HC = HEADS // KC
    GI = 8
    AHEAD, BEHIND = 6, 2
    DST_AHEAD = GI - 4
    with ExitStack() as ctx:
        def sb(name, shape, dt=F32):
            return ctx.enter_context(nc.sbuf_tensor(name, shape, dt))

        def sem(name):
            return ctx.enter_context(nc.semaphore(name))

        src = [sb(f"src{r}", [P, 2], I32) for r in range(GI)]
        dst = [sb(f"dst{r}", [P, 2], I32) for r in range(GI)]
        xg = [sb(f"xg{r}", [P, D]) for r in range(GI)]
        xgT = [sb(f"xgT{u}", [P, KC, P]) for u in range(2)]
        gate = [sb(f"gate{u}", [P, FF]) for u in range(2)]
        hid = [sb(f"hid{u}", [P, FF]) for u in range(2)]
        hidT = [sb(f"hidT{u}", [P, KC, P]) for u in range(2)]
        y = [sb(f"y{r}", [P, D]) for r in range(GI)]
        sums = sb("sums", [P, HEADS * TOK // P])
        inv = sb("inv_sums", [P, HEADS * TOK // P])
        o_in = sb("o_in", [P, KC, BLK])
        inv_in = sb("inv_in", [P, KC, BLK])
        oT = [sb(f"oT{u}", [P, KC, P]) for u in range(2)]
        pP = [ctx.enter_context(nc.psum_tensor(f"pP{u}", [P, D], F32)) for u in range(2)]
        pXT = ctx.enter_context(nc.psum_tensor("pXT", [P, KC, P], F32))
        pHT = ctx.enter_context(nc.psum_tensor("pHT", [P, KC, P], F32))
        pGU = [ctx.enter_context(nc.psum_tensor(f"pGU{u}", [P, 2 * FF], F32)) for u in range(2)]
        pY = [ctx.enter_context(nc.psum_tensor(f"pY{u}", [P, 512], F32)) for u in range(2)]
        src_loaded = [sem(f"src_loaded{r}") for r in range(GI)]
        dst_loaded = [sem(f"dst_loaded{r}") for r in range(GI)]
        gathered = [sem(f"gathered{r}") for r in range(GI)]
        scattered = [sem(f"scattered{r}") for r in range(GI)]
        passed = sem("passed")
        xT_done = sem("xgT_done")
        xT_copied = sem("xgT_copied")
        gu_done = sem("gu_done")
        gate_done = sem("gate_done")
        hid_done = sem("hid_done")
        hidT_done = sem("hidT_done")
        hidT_copied = sem("hidT_copied")
        y_done = sem("y_done")
        y_copied = sem("y_copied")
        sums_loaded = sem("sums_loaded")
        inv_done = sem("inv_done")
        inv_stored = sem("inv_stored")
        block_loaded = sem("block_loaded")
        oT_done = sem("oT_done")
        proj_done = sem("proj_done")
        proj_added = sem("proj_added")
        LOADS = 16 * (1 + 2 * KC)
        FREE = 2
        block = ctx.enter_context(nc.Block())

        def every_tile(eng, step):
            for n in range(GI):
                step(n, n, 0)
            with eng.Fori(0, SLOT_TILES // GI - 2) as i:
                for r in range(GI):
                    step(GI * i + GI + r, r, i + 1)
            for r in range(GI):
                step(SLOT_TILES - GI + r, r, SLOT_TILES // GI - 1)

        assert NBLK == SLOT_TILES // GI - 1 and GI == 2 * JT

        def below(n, k):
            return isinstance(n, int) and n < k

        def last_ones(n, k):
            return isinstance(n, int) and n >= SLOT_TILES - k

        @block.sync
        def _(sp):
            def load(ring, loaded, n, r):
                sp.dma_start(ring[r][:, :], slot_d[bass.ds(n * P, P), :]).then_inc(loaded[r], 16)

            sp.dma_start(sums[:, :], sums_d.rearrange("h (a t) -> (h a) t", a=P // HEADS)).then_inc(sums_loaded, 16)
            for n in range(GI):
                load(src, src_loaded, n, n)
                load(dst, dst_loaded, n, n)
            sp.wait_ge(inv_done, 1)
            sp.dma_start(inv_d.rearrange("h (a t) -> (h a) t", a=P // HEADS), inv[:, :]).then_inc(inv_stored, 16)
            sp.wait_ge(inv_stored, 16)

            def load_block(m):
                sp.dma_start(acc[:, bass.ds(m * JT, JT), :], x_t[bass.ds(m, 1)].squeeze(0)).then_inc(block_loaded, 16)
                cols = bass.ds(m * BLK, BLK)
                for c in range(KC):
                    heads = slice(c * HC, (c + 1) * HC)
                    sp.dma_start(o_in[:, c, :], o_d[heads, :, cols]).then_inc(block_loaded, 16)
                    sp.dma_start(inv_in[:, c, :], inv_d[heads, cols].unsqueeze(1).to_broadcast([HC, HD, BLK])
                                 ).then_inc(block_loaded, 16)

            load_block(0)

            def step(n, r, k):
                if r == GI - 1 and not below(n, GI) and not last_ones(n, 1):
                    sp.wait_ge(oT_done, JT * k)
                    load_block(k)
                if not last_ones(n, GI):
                    sp.wait_ge(gathered[r], 16 * (k + 1))
                    load(src, src_loaded, n + GI, r)
                if not below(n, GI - DST_AHEAD) and not last_ones(n, DST_AHEAD):
                    q, m = (r + DST_AHEAD) % GI, k + (r + DST_AHEAD) // GI
                    sp.wait_ge(scattered[q], 16 * m)
                    load(dst, dst_loaded, n + DST_AHEAD, q)

            every_tile(sp, step)

        @block.gpsimd
        def _(pool):
            def gather(n, r, k):
                pool.wait_ge(src_loaded[r], 16 * (k + 1))
                if not below(n, GI):
                    wait_alone(pool, xT_done, n - GI + 1, passed)
                nc.gpsimd.indirect_dma_start(xg[r][:, :], None, xn_d,
                                             bass.IndirectOffsetOnAxis(src[r][:, 0:1].bitcast(U32), 0),
                                             bounds_check=TOK - 1).then_inc(gathered[r], 16)

            for n in range(AHEAD):
                gather(n, n, 0)

            def scatter(n, r, k):
                pool.wait_ge(y_copied, n + 1)
                wait_alone(pool, dst_loaded[r], 16 * (k + 1), passed)
                nc.gpsimd.indirect_dma_start(y_d, bass.IndirectOffsetOnAxis(dst[r][:, 1:2].bitcast(U32), 0),
                                             y[r][:, :], None, bounds_check=2 * TOK - 1,
                                             oob_is_err=False).then_inc(scattered[r], 16)

            def step(n, r, k):
                if not last_ones(n, AHEAD):
                    gather(n + AHEAD, (r + AHEAD) % GI, k + (r + AHEAD) // GI)
                if not below(n, BEHIND):
                    scatter(n - BEHIND, (r - BEHIND) % GI, k + (r - BEHIND) // GI)

            every_tile(pool, step)
            for n in range(SLOT_TILES - BEHIND, SLOT_TILES):
                scatter(n, n % GI, n // GI)
            for r in range(GI):
                pool.wait_ge(scattered[r], 16 * SLOT_TILES // GI)

        @block.scalar
        def _(act):
            def x_copy(n, u):
                act.wait_ge(xT_done, n + 1)
                if not below(n, 2):
                    act.wait_ge(gu_done, n - 1)
                nc.scalar.activation(xgT[u][:, :, :], pXT[:, :, :], ACT.Copy).then_inc(xT_copied, 1)

            def step(n, r, k):
                u = r % 2
                act.wait_ge(gu_done, n + 1)
                if not below(n, 2):
                    act.wait_ge(hid_done, n - 1)
                nc.scalar.activation(gate[u][:, :], pGU[u][:, 0:FF], ACT.Silu).then_inc(gate_done, 1)
                if not last_ones(n, 1):
                    x_copy(n + 1, 1 - u)
                if not below(n, 1):
                    y_copy(n - 1, (r - 1) % GI, k + (r - 1) // GI)

            def y_copy(n, r, k):
                act.wait_ge(y_done, n + 1)
                if not below(n, GI):
                    act.wait_ge(scattered[r], 16 * k)
                nc.scalar.activation(y[r][:, :], pY[r % 2][:, 0:D], ACT.Copy).then_inc(y_copied, 1)

            x_copy(0, 0)
            every_tile(act, step)
            y_copy(SLOT_TILES - 1, GI - 1, SLOT_TILES // GI - 1)

        @block.vector
        def _(dve):
            dve.sem_inc(proj_added, FREE)
            dve.wait_ge(sums_loaded, 16)
            nc.vector.reciprocal(inv[:, :], sums[:, :]).then_inc(inv_done, 1)

            def divide(q, k):
                t = JT * (k - 1) + q
                if q == 0:
                    dve.wait_ge(block_loaded, LOADS * k)
                dve.wait_ge(proj_done, FREE + t - 1)
                cols = slice(q * P, (q + 1) * P)
                nc.vector.tensor_tensor(oT[q % 2][:, :, :], o_in[:, :, cols], inv_in[:, :, cols], ALU.mult).then_inc(oT_done, 1)

            def add(q, k):
                t = JT * (k - 1) + q
                dve.wait_ge(proj_done, FREE + t + 1)
                part = acc[:, bass.ds(t, 1), :].squeeze(1)
                nc.vector.tensor_tensor(part, pP[q % 2][:, :], part, ALU.add).then_inc(proj_added, 1)

            def step(n, r, k):
                u = r % 2
                hidden(n, r, k, u)
                if not below(n, GI):
                    if r % 2 == 0:
                        divide(r // 2, k)
                    else:
                        add(r // 2, k)

            def hidden(n, r, k, u):
                dve.wait_ge(gate_done, n + 1)
                if not below(n, 2):
                    dve.wait_ge(hidT_done, n - 1)
                nc.vector.tensor_tensor(hid[u][:, :], pGU[u][:, FF:2 * FF], gate[u][:, :], ALU.mult).then_inc(hid_done, 1)
                dve.wait_ge(hidT_done, n + 1)
                if not below(n, 2):
                    dve.wait_ge(y_done, n - 1)
                nc.vector.tensor_copy(hidT[u][:, :, :], pHT[:, :, :]).then_inc(hidT_copied, 1)

            every_tile(dve, step)

        @block.tensor
        def _(pe):
            pe.sem_inc(proj_done, FREE)
            def transpose_x(n, r, k):
                pe.wait_ge(gathered[r], 16 * (k + 1))
                if not below(n, 1):
                    pe.wait_ge(xT_copied, n)
                for c in range(KC):
                    last = nc.tensor.transpose(pXT[:, c, :], xg[r][:, c * P:(c + 1) * P], ident[:, :])
                last.then_inc(xT_done, 1)

            def gate_up_half(n, u, e, c):
                if c == 0:
                    pe.wait_ge(xT_copied, n + 1)
                    if not below(n, 2):
                        pe.wait_ge(hid_done, n - 1)
                last = nc.tensor.matmul(pGU[u][:, :], xgT[u][:, c, :], w_gu[:, c, bass.ds(e * (2 * FF), 2 * FF)],
                                        start=c == 0, stop=c == KC - 1)
                if c == KC - 1:
                    last.then_inc(gu_done, 1)

            def transpose_h(n, u):
                pe.wait_ge(hid_done, n + 1)
                if not below(n, 1):
                    pe.wait_ge(hidT_copied, n)
                for c in range(KC):
                    last = nc.tensor.transpose(pHT[:, c, :], hid[u][:, c * P:(c + 1) * P], ident[:, :])
                last.then_inc(hidT_done, 1)

            def down_product(n, u, e):
                pe.wait_ge(hidT_copied, n + 1)
                if not below(n, 2):
                    pe.wait_ge(y_copied, n - 1)
                for c in range(KC):
                    last = nc.tensor.matmul(pY[u][:, 0:D], hidT[u][:, c, :], w_dn[:, c, bass.ds(e * D, D)],
                                            start=c == 0, stop=c == KC - 1)
                last.then_inc(y_done, 1)

            def expert_of(n):
                return nc.tensor.value_load(tile_expert[0:1, bass.ds(n, 1)], min_val=0, max_val=EXPERTS - 1)

            transpose_x(0, 0, 0)

            def step(n, r, k):
                u = r % 2
                e = expert_of(n)
                gate_up_half(n, u, e, 0)
                if not below(n, 1):
                    transpose_h(n - 1, 1 - u)
                gate_up_half(n, u, e, 1)
                if not last_ones(n, 1):
                    transpose_x(n + 1, (r + 1) % GI, k + (r + 1) // GI)
                if not below(n, 1):
                    down_product(n - 1, 1 - u, expert_of(n - 1))
                if r % 2 == 1 and not below(n, GI):
                    project(r // 2, k)

            def project(q, k):
                t = JT * (k - 1) + q
                pe.wait_ge(oT_done, t + 1)
                pe.wait_ge(proj_added, FREE + t - 1)
                for c in range(KC):
                    last = nc.tensor.matmul(pP[q % 2][:, :], oT[q % 2][:, c, :], w_o_sb[:, c, :],
                                            start=c == 0, stop=c == KC - 1)
                last.then_inc(proj_done, 1)

            every_tile(pe, step)
            transpose_h(SLOT_TILES - 1, 1)
            down_product(SLOT_TILES - 1, 1, expert_of(SLOT_TILES - 1))


def combine(nc, y_d, weights, acc, out):
    RB = 4
    y_t = y_d.rearrange("(r n j p) d -> r n p j d", r=2, j=JT, p=P)
    out_t = out.rearrange("b (n j p) d -> (b n) p j d", j=JT, p=P)
    with ExitStack() as ctx:
        def sem(name):
            return ctx.enter_context(nc.semaphore(name))

        ys = [[ctx.enter_context(nc.sbuf_tensor(f"ys{q}_{r}", [P, JT, D], F32)) for r in range(2)] for q in range(RB)]
        y_loaded = [sem(f"y_loaded{q}") for q in range(RB)]
        first_added = sem("first_added")
        added = sem("added")
        stored = sem("stored")
        block = ctx.enter_context(nc.Block())

        def every_block(eng, step):
            for n in range(RB):
                step(n, n, 0)
            with eng.Fori(0, NBLK // RB - 1) as i:
                for q in range(RB):
                    step(RB * i + RB + q, q, i + 1)

        @block.sync
        def _(sp):
            def step(n, q, k):
                if not isinstance(n, int):
                    sp.wait_ge(added, n - RB + 1)
                for r in range(2):
                    sp.dma_start(ys[q][r][:, :, :], y_t[r, bass.ds(n, 1)].squeeze(0)).then_inc(y_loaded[q], 16)

            every_block(sp, step)

        @block.vector
        def _(dve):
            def step(n, q, k):
                dve.wait_ge(y_loaded[q], 32 * (k + 1))
                for r in range(2):
                    for j in range(JT):
                        tile = acc[:, bass.ds(n * JT + j, 1), :].squeeze(1)
                        last = nc.vector.scalar_tensor_tensor(tile, ys[q][r][:, j, :],
                                                              weights[:, r, bass.ds(n * JT + j, 1)], tile,
                                                              ALU.mult, ALU.add)
                    if r == 0:
                        last.then_inc(first_added, 1)
                        dve.wait_ge(first_added, n + 1)
                last.then_inc(added, 1)

            every_block(dve, step)

        @block.scalar
        def _(act):
            def step(n, q, k):
                act.wait_ge(added, n + 1)
                act.dma_start(out_t[bass.ds(n, 1)].squeeze(0), acc[:, bass.ds(n * JT, JT), :]).then_inc(stored, 16)

            every_block(act, step)
            act.wait_ge(stored, 16 * NBLK)


def program(nc, x, w_qkv, w_o, gate_w, gate_up, down, out):
    xn_d = nc.dram_tensor("xn_d", (TOK, D), F32, kind="Internal").ap()
    split_d = nc.dram_tensor("split_d", (3, 2, HEADS * HD, TOK), BF16, kind="Internal").ap()
    v_d = nc.dram_tensor("v_d", (HGS, P, TOK // P, GH * VW), F32, kind="Internal").ap()
    o_d = nc.dram_tensor("o_d", (HEADS, HD, TOK), F32, kind="Internal").ap()
    sums_d = nc.dram_tensor("sums_d", (HEADS, TOK), F32, kind="Internal").ap()
    inv_d = nc.dram_tensor("inv_d", (HEADS, TOK), F32, kind="Internal").ap()
    slot_d = nc.dram_tensor("slot_d", (SLOT_TILES * P, 2), I32, kind="Internal").ap()
    y_d = nc.dram_tensor("y_d", (2 * TOK, D), F32, kind="Internal").ap()
    with ExitStack() as ctx:
        def sb(name, shape, dt=F32):
            return ctx.enter_context(nc.sbuf_tensor(name, shape, dt))

        ident = sb("ident", [P, P])
        weights = sb("weights", [P, 2, TOK // P])
        tile_expert = sb("tile_expert", [1, SLOT_TILES], I32)
        w_o_sb = sb("w_o_sb", [P, KC, D])
        w_gu = sb("w_gu", [P, KC, EXPERTS * 2 * FF])
        w_dn = sb("w_dn", [P, KC, EXPERTS * D])
        with ExitStack() as upto_attention:
            def sb1(name, shape, dt=F32):
                return upto_attention.enter_context(nc.sbuf_tensor(name, shape, dt))

            slots = sb1("slots", [P, TOK // P, 2], I32)
            tokens = sb1("tokens", [P, TOK // P, 2, 2], I32)
            first_ops = FirstOperands(nc, upto_attention)
            with nc.sbuf_tensor("logits", [P, TOK // P, EXPERTS], F32) as logits:
                layernorm_qkv(nc, x, w_qkv, gate_w, xn_d, split_d, v_d, logits, ident)
                route(nc, logits, weights, slots, tokens, tile_expert, slot_d, first_ops, split_d, v_d)
            attention(nc, first_ops, split_d, v_d, o_d, sums_d, slots, tokens, slot_d,
                      [(w_o_sb, w_o), (w_gu, gate_up), (w_dn, down)])
        with nc.sbuf_tensor("acc", [P, TOK // P, D], F32) as acc:
            experts(nc, xn_d, slot_d, tile_expert, w_gu, w_dn, y_d, ident, x, o_d, sums_d, inv_d, w_o_sb, acc)
            combine(nc, y_d, weights, acc, out)


_INS = ["L0_attn_x", "L0_attn_w_qkv", "L0_attn_w_o", "L0_ffn_gate_w", "L0_ffn_gate_up_proj", "L0_ffn_down_proj"]


def kernel(**inputs):
    import numpy as np
    import concourse.bacc as bacc
    from concourse import mybir as mb
    from concourse.bass_utils import run_bass_kernel_spmd as run

    nc = bacc.Bacc("TRN2", target_bir_lowering=False, num_devices=1)
    arrays, args = {}, []
    for name in _INS:
        a = np.ascontiguousarray(inputs[name])
        arrays[f"in_{name}"] = a
        args.append(nc.dram_tensor(f"in_{name}", a.shape, mb.dt.from_np(a.dtype), kind="ExternalInput").ap())
    out = nc.dram_tensor("out_dram", (BATCH, T, D), F32, kind="ExternalOutput").ap()
    program(nc, *args, out)
    return run(nc, [arrays], core_ids=[0]).results[0]["out_dram"]
```
